# Optimizing a Trainium2 kernel written in Bass

```python
import numpy as np
import jax
import jax.numpy as jnp

def _softmax(x, axis=-1):
    return jax.nn.softmax(x, axis=axis)

def _gelu(x):
    return jax.nn.gelu(x, approximate=True)

def _silu(x):
    return jax.nn.silu(x)

def _sigmoid(x):
    return jax.nn.sigmoid(x)

def _layernorm(x, axis=-1, eps=1e-05):
    m = jnp.mean(x, axis=axis, keepdims=True)
    v = jnp.var(x, axis=axis, keepdims=True)
    return (x - m) / jnp.sqrt(v + eps)

def _scatter_add(tgt, idx, src, axis=0):
    return tgt.at[idx].add(src)

def _segment_sum(src, seg, n):
    return jax.ops.segment_sum(src, seg, n)
kernel_name = 'mk_flamingo_gated_d1_seqx_r4_16dc65'

def setup_inputs(seed: int=0):
    np.random.seed(seed)
    _w = jnp.asarray

    def _rec_inputs():
        import jax
        import jax.numpy as jnp
        _rk = jax.random.key(seed)
        x = 7.22e-05 + 1 * jax.random.normal(jax.random.fold_in(_rk, 1), (8, 256, 512), jnp.float32)
        _lenS = 256 - jax.random.randint(jax.random.fold_in(_rk, 7), (8,), 0, max(1, 256 // 4) + 1, jnp.int32)
        _lenS2 = 256 - jax.random.randint(jax.random.fold_in(_rk, 8), (8,), 0, max(1, 256 // 4) + 1, jnp.int32)
        _ctx_2048P = jax.random.normal(jax.random.fold_in(_rk, 11), (8, 16, 512), jnp.float32)
        _ctx_2048c = jax.random.dirichlet(jax.random.fold_in(_rk, 511), 0.3 * jnp.ones((16,), jnp.float32), (8, 256))
        _ctx_2048t = jnp.einsum('bsk,bkd->bsd', _ctx_2048c, _ctx_2048P)
        _ctx_2048t = _ctx_2048t * jax.lax.rsqrt(jnp.mean(jnp.square(_ctx_2048t)) + 1e-12) * 0.953939
        ctx_2048 = 4.13588e-05 + 0.999923 * (_ctx_2048t + 0.3 * jax.random.normal(jax.random.fold_in(_rk, 611), (8, 256, 512), jnp.float32))
        _validS = jnp.arange(256)[None, :] < _lenS[:, None]
        _validS2 = jnp.arange(256)[None, :] < _lenS2[:, None]
        _causal = jnp.tril(jnp.ones((256, 256), dtype=bool))
        mask_SxS2_bc0 = jnp.logical_not(jnp.broadcast_to(_validS2[0:1, :], (256, 256)))
        mask_BxS2_bk0 = jnp.logical_not(jnp.broadcast_to(_validS2[:, :], (8, 256)))
        _g = jax.random.normal(jax.random.fold_in(_rk, 9001), (2, 1), jnp.float32)
        _g = jnp.sign(_g) * jnp.maximum(jnp.abs(_g), 1.0) + (_g == 0) * 1.0
        g_xattn = _g[0]
        g_ffn = _g[1]
        return (x, ctx_2048, mask_SxS2_bc0, mask_BxS2_bk0, g_xattn, g_ffn)
    x, ctx_2048, mask_SxS2_bc0, mask_BxS2_bk0, g_xattn, g_ffn = _rec_inputs()

    def _L0_xattn_setup():
        import jax, jax.numpy as jnp
        import numpy as np
        B, LQ, LKV = (4, 256, 256)
        HID, H, G = (512, 32, 8)
        HD = HID // H
        HPG = H // G
        key = jax.random.key(seed)
        ks = jax.random.split(key, 10)
        s = 0.02
        inp = {'X': jax.random.normal(ks[0], (B, LQ, HID), jnp.float32), 'encoder_output': jax.random.normal(ks[1], (B, LKV, HID), jnp.float32), 'causal_mask': jnp.triu(jnp.ones((LQ, LKV), bool), 1), 'padding_mask': jnp.zeros((B, LKV), bool).at[B // 2:, LKV - LKV // 4:].set(True), 'Wq': jax.random.normal(ks[2], (HID, HID), jnp.float32) * s, 'bq': jnp.zeros((HID,), jnp.float32), 'Wk': jax.random.normal(ks[3], (G * HD, HID), jnp.float32) * s, 'bk': jnp.zeros((G * HD,), jnp.float32), 'Wv': jax.random.normal(ks[4], (G * HD, HID), jnp.float32) * s, 'bv': jnp.zeros((G * HD,), jnp.float32), 'Wo': jax.random.normal(ks[5], (HID, HID), jnp.float32) * s, 'bo': jnp.zeros((HID,), jnp.float32)}
        return inp
    _L0_xattn_all = _L0_xattn_setup()
    _L0_xattn_in = {k: v for k, v in _L0_xattn_all.items() if k in ('Wq', 'bq', 'Wk', 'bk', 'Wv', 'bv', 'Wo', 'bo')}
    del _L0_xattn_all

    def _L0_ffn_setup():
        import jax, jax.numpy as jnp
        import numpy as np
        B, S, H, I = (1, 64, 512, 1536)

        def _quantized_matmul(x, w, scale):
            wq = w.astype(jnp.float8_e4m3fn).astype(x.dtype)
            y = jnp.einsum('bsi,io->bso', x, wq)
            return y * scale
        key = jax.random.key(seed)
        ks = jax.random.split(key, 7)
        return {'x': jax.random.normal(ks[0], (B, S, H), dtype=jnp.float32), 'gate_w': jax.random.normal(ks[1], (H, I), dtype=jnp.float32) * 0.02, 'up_w': jax.random.normal(ks[2], (H, I), dtype=jnp.float32) * 0.02, 'down_w': jax.random.normal(ks[3], (I, H), dtype=jnp.float32) * 0.02, 'gate_scale': jax.random.uniform(ks[4], (I,), dtype=jnp.float32, minval=0.5, maxval=1.5), 'up_scale': jax.random.uniform(ks[5], (I,), dtype=jnp.float32, minval=0.5, maxval=1.5), 'down_scale': jax.random.uniform(ks[6], (H,), dtype=jnp.float32, minval=0.5, maxval=1.5)}
    _L0_ffn_all = _L0_ffn_setup()
    _L0_ffn_in = {k: v for k, v in _L0_ffn_all.items() if k in ('gate_w', 'up_w', 'down_w', 'gate_scale', 'up_scale', 'down_scale')}
    del _L0_ffn_all
    return {'x': x, 'ctx_2048': ctx_2048, 'mask_SxS2_bc0': mask_SxS2_bc0, 'mask_BxS2_bk0': mask_BxS2_bk0, 'g_xattn': g_xattn, 'g_ffn': g_ffn, 'L0_xattn_Wq': _L0_xattn_in['Wq'], 'L0_xattn_bq': _L0_xattn_in['bq'], 'L0_xattn_Wk': _L0_xattn_in['Wk'], 'L0_xattn_bk': _L0_xattn_in['bk'], 'L0_xattn_Wv': _L0_xattn_in['Wv'], 'L0_xattn_bv': _L0_xattn_in['bv'], 'L0_xattn_Wo': _L0_xattn_in['Wo'], 'L0_xattn_bo': _L0_xattn_in['bo'], 'L0_ffn_gate_w': _L0_ffn_in['gate_w'], 'L0_ffn_up_w': _L0_ffn_in['up_w'], 'L0_ffn_down_w': _L0_ffn_in['down_w'], 'L0_ffn_gate_scale': _L0_ffn_in['gate_scale'], 'L0_ffn_up_scale': _L0_ffn_in['up_scale'], 'L0_ffn_down_scale': _L0_ffn_in['down_scale']}

def reference(x, ctx_2048, mask_SxS2_bc0, mask_BxS2_bk0, g_xattn, g_ffn, L0_xattn_Wq, L0_xattn_bq, L0_xattn_Wk, L0_xattn_bk, L0_xattn_Wv, L0_xattn_bv, L0_xattn_Wo, L0_xattn_bo, L0_ffn_gate_w, L0_ffn_up_w, L0_ffn_down_w, L0_ffn_gate_scale, L0_ffn_up_scale, L0_ffn_down_scale):
    import jax
    import jax.numpy as jnp

    def _L0_xattn_ref(X, encoder_output, causal_mask, padding_mask, Wq, bq, Wk, bk, Wv, bv, Wo, bo):
        import jax, jax.numpy as jnp
        import numpy as np
        B, LQ, LKV = (4, 256, 256)
        HID, H, G = (512, 32, 8)
        HD = HID // H
        HPG = H // G
        b = X.shape[0]
        q = X @ Wq.T + bq
        k = encoder_output @ Wk.T + bk
        v = encoder_output @ Wv.T + bv
        q = q.reshape(b, LQ, G, HPG, HD).transpose(0, 2, 3, 1, 4)
        k = k.reshape(b, LKV, G, HD).transpose(0, 2, 1, 3)
        v = v.reshape(b, LKV, G, HD).transpose(0, 2, 1, 3)
        scores = jnp.einsum('bgrqd,bgkd->bgrqk', q, k) / jnp.sqrt(jnp.float32(HD))
        scores = jnp.where(causal_mask[None, None, None, :, :], -jnp.inf, scores)
        scores = jnp.where(padding_mask[:, None, None, None, :], -jnp.inf, scores)
        w = jax.nn.softmax(scores, axis=-1)
        out = jnp.einsum('bgrqk,bgkd->bgrqd', w, v)
        out = out.reshape(b, H, LQ, HD).transpose(0, 2, 1, 3).reshape(b, LQ, HID)
        return out @ Wo.T + bo

    def _L0_ffn_ref(x, gate_w, up_w, down_w, gate_scale, up_scale, down_scale):
        import jax, jax.numpy as jnp
        import numpy as np
        B, S, H, I = (1, 64, 512, 1536)

        def _quantized_matmul(x, w, scale):
            wq = w.astype(jnp.float8_e4m3fn).astype(x.dtype)
            y = jnp.einsum('bsi,io->bso', x, wq)
            return y * scale
        gate = jax.nn.silu(_quantized_matmul(x, gate_w, gate_scale))
        up = _quantized_matmul(x, up_w, up_scale)
        fuse = gate * up
        return _quantized_matmul(fuse, down_w, down_scale)
    x = x + jnp.tanh(g_xattn[0]) * _L0_xattn_ref(_layernorm(x, axis=-1), ctx_2048, mask_SxS2_bc0, mask_BxS2_bk0, L0_xattn_Wq, L0_xattn_bq, L0_xattn_Wk, L0_xattn_bk, L0_xattn_Wv, L0_xattn_bv, L0_xattn_Wo, L0_xattn_bo)
    x = x + jnp.tanh(g_ffn[0]) * _L0_ffn_ref(_layernorm(x, axis=-1), L0_ffn_gate_w, L0_ffn_up_w, L0_ffn_down_w, L0_ffn_gate_scale, L0_ffn_up_scale, L0_ffn_down_scale)
    return x

_drawn_inputs = setup_inputs


def setup_inputs(seed=0):
    import zlib

    import numpy as np

    out = dict(_drawn_inputs(seed))
    spreads = {'L0_xattn_bq': (0.0, 0.8),
     'L0_xattn_bk': (0.0, 0.8),
     'L0_xattn_bv': (0.0, 0.1),
     'L0_xattn_bo': (0.0, 0.1)}
    factors = {'L0_xattn_Wq': 8.0, 'L0_xattn_Wk': 8.0}
    for name, (base, spread) in spreads.items():
        noise = np.random.default_rng([zlib.crc32(name.encode()), seed]).standard_normal(out[name].shape)
        drawn = base * np.exp(spread * noise) if base else spread * noise
        out[name] = jnp.asarray(drawn.astype(out[name].dtype))
    for name, factor in factors.items():
        out[name] = (out[name] * factor).astype(out[name].dtype)
    return out
```

```python
import concourse.bass as bass
from concourse import mybir
from contextlib import ExitStack

NB, L, D = 8, 256, 512
H, G, HD = 32, 8, 16
HPG = H // G
F = 1536
P = 128
TT = L // P
KT = D // P
FT = F // P
PAIRS = H // 2
KV = G * HD

SX = 4.0
SWQK = 16.0
SWVO = 256.0
SQK = SX * SWQK
SSC = SQK * SQK * 4.0
SM = 2048.0
SA = 64.0
SF = 64.0
BIG = 1.0e30

STEPS = 32
PIECES = {
    0: [("down_a", 0)], 1: [("down_b", 0)], 2: [("kv", 0), ("recip", 0)], 3: [],
    4: [("down_a", 1), ("stats1", 0)], 5: [("down_b", 1), ("shift1", 0)],
    6: [("spread", 0), ("spread", 1)], 7: [("split_att", 0), ("split_att", 1), ("norm1", 0)],
    8: [("xT", 0)], 9: [("out", 0)], 10: [("xT", 1)], 11: [("out", 1), ("stats2", 0)],
    12: [("q", 0)], 13: [("mrow", 1), ("shift2", 0)], 14: [("q", 1)], 15: [("norm2", 0)],
    16: [("x2T", 0)], 17: [("x2T", 1), ("cT", 0)], 18: [("gu", 0)], 19: [("gu", 1)],
    20: [("gu", 2), ("cT", 1), ("fsplit", 0)], 21: [("gu", 3), ("fsplit", 1)], 22: [("gu", 4), ("fsplit", 2)],
    23: [("gu", 5), ("fsplit", 3)], 24: [("gu", 6), ("fsplit", 4)], 25: [("gu", 7), ("fsplit", 5)],
    26: [("gu", 8), ("fsplit", 6)], 27: [("gu", 9), ("fsplit", 7)], 28: [("gu", 10), ("fsplit", 8)],
    29: [("mrow", 0), ("fsplit", 9)], 30: [("gu", 11), ("fsplit", 10)], 31: [],
}
LATE = [("fsplit", 11)]
OFF = {"down_a": -2, "down_b": -2, "kv": 1, "recip": -1, "stats1": 2, "shift1": 2, "norm1": 2, "spread": -1,
       "split_att": -1, "xT": 2, "out": -1, "q": 2, "stats2": -1, "shift2": -1, "norm2": -1, "x2T": -1, "cT": 2,
       "gu": -1, "fsplit": -1}
A_USES = 7
C_USES = 20
SETUP_USES = 12


def past(eng, sem, count):
    if not isinstance(count, int) or count > 0:
        eng.wait_ge(sem, count)


def place(j):
    at = L * (2 * (j % 2) + j // 2)
    return slice(at, at + L)


def there(r, off):
    return not isinstance(r, int) or 0 <= r + off < NB


def xattn_ffn(nc, x, ctx, mask_qk, mask_pad, g_att, g_ffn, Wq, bq, Wk, bk, Wv, bv, Wo, bo,
              gate_w, up_w, down_w, gate_s, up_s, down_s, ident_in, spread_in, out):
    f32, f16, f8, u8 = mybir.dt.float32, mybir.dt.float16, mybir.dt.float8e4, mybir.dt.uint8
    ALU, ACT, AX = mybir.AluOpType, mybir.ActivationFunctionType, mybir.AxisListType
    es = ExitStack()
    with es:
        def sb(name, shape, dt):
            return es.enter_context(nc.sbuf_tensor(name, shape, dt))

        def sem(name):
            return es.enter_context(nc.semaphore(name))

        wq_h, wq_l = sb("wq_h", [P, KT, D], f16), sb("wq_l", [P, KT, D], f16)
        wo_h, wo_l = sb("wo_h", [P, KT, D], f16), sb("wo_l", [P, KT, D], f16)
        wk_h, wk_l = sb("wk_h", [P, KT, KV], f16), sb("wk_l", [P, KT, KV], f16)
        wv_h, wv_l = sb("wv_h", [P, KT, KV], f16), sb("wv_l", [P, KT, KV], f16)
        wg8, wu8, wd8 = sb("wg8", [P, KT, F], f8), sb("wu8", [P, KT, F], f8), sb("wd8", [P, FT, D], f8)
        ident, spread = sb("ident", [P, P], f32), sb("spread", [2 * H, KT, P], f16)
        bq_c, bk_c, bv_b = sb("bq_c", [P, KT], f32), sb("bk_c", [P, 1], f32), sb("bv_b", [P, KV], f32)
        tg, tgo, tgf = sb("tg", [P, 2], f32), sb("tgo", [P, 1], f32), sb("tgf", [P, 1], f32)
        tgbo, dsb = sb("tgbo", [P, D], f32), sb("dsb", [P, D], f32)
        gs_c = sb("gs_c", [P, FT], f32)
        tanh_s, fuse_s = sb("tanh_s", [P, FT], f32), sb("fuse_s", [P, FT], f32)
        mhalf = sb("mhalf", [P, 2], f32)
        mask_u8 = sb("mask_u8", [P, TT, L], u8)
        mask_q, mask_k = sb("mask_q", [P, TT, L], f32), sb("mask_k", [P, TT, L], f32)
        padr_u8 = sb("padr_u8", [P, NB, L], u8)
        padc_u8, padc_all = sb("padc_u8", [NB * TT, P], u8), sb("padc_all", [P, NB * TT], f32)
        row_bq = NB * TT
        row_bk, row_gs = row_bq + KT, row_bq + KT + 1
        row_us = row_gs + FT
        rows_in = sb("rows_in", [row_us + FT, P], f32)
        xin, xn = sb("xin", [P, TT, D], f32), sb("xn", [P, TT, D], f32)
        cin = sb("cin", [P, TT, D], f32)
        xh, xl = sb("xh", [P, KT, L], f16), sb("xl", [P, KT, L], f16)
        ch, cl = sb("ch", [P, KT, L], f16), sb("cl", [P, KT, L], f16)
        qh, ql = sb("qh", [P, KT, L], f16), sb("ql", [P, KT, L], f16)
        kh, kl = sb("kh", [P, L], f16), sb("kl", [P, L], f16)
        qs = [sb(f"qs{i}", [P, PAIRS, L], f16) for i in range(2)]
        ks = [sb(f"ks{i}", [P, G, L], f16) for i in range(2)]
        va = [sb(f"va{i}", [P, TT, G, 32], f32) for i in range(2)]
        mq = [sb(f"mq{i}", [P, TT, L], f32) for i in range(2)]
        padrow = sb("padrow", [P, L], f32)
        padc = [sb(f"padc{i}", [P, TT], f32) for i in range(2)]
        mx, junk = sb("mx", [P, TT, H], f32), sb("junk", [P, 2 * HPG, L], mybir.dt.bfloat16)
        nm_h, nm_l = sb("nm_h", [H // 2, L], f16), sb("nm_l", [H // 2, L], f16)
        ws = sb("ws", [P, 4, HPG, L], f32)
        un = sb("un", [P, G, L], f32)
        att_u, att, den, rden = sb("att_u", [P, KT, L], f32), sb("att", [P, KT, L], f32), sb("den", [H, L], f32), sb("rden", [H, L], f32)
        rd = sb("rd", [2 * H, L], f16)
        at_h, at_l = sb("at_h", [P, KT, L], f16), sb("at_l", [P, KT, L], f16)
        xb, x2, x2n = sb("xb", [P, TT, D], f32), sb("x2", [P, TT, D], f32), sb("x2n", [P, TT, D], f32)
        h2_h, h2_l = sb("h2_h", [P, KT, L], f16), sb("h2_l", [P, KT, L], f16)
        th, ga = sb("th", [P, 2, L], f32), sb("ga", [P, L], f32)
        ff = sb("ff", [P, 4, L], f32)
        f_h, f_l = sb("f_h", [P, FT, L], f16), sb("f_l", [P, FT, L], f16)
        yt = sb("yt", [P, TT, D], f32)
        bst = [sb(f"bst{i}", [P, TT, 6], f32) for i in range(2)]
        mv = [sb(f"mv{i}", [P, TT, 2], f32) for i in range(2)]
        ve = [sb(f"ve{i}", [P, TT], f32) for i in range(2)]
        rs = [sb(f"rs{i}", [P, TT], f32) for i in range(2)]
        nb_ = [sb(f"nb{i}", [P, TT], f32) for i in range(2)]

        st_q = un[:, :, :].rearrange("p (t a) l -> p t (a l)", t=KT)
        st_k = att_u[:, 0:2, :].rearrange("p a l -> p (a l)")
        st_v = att_u[:, 2:4, :].rearrange("p a l -> p (a l)")
        mask_f = att[:, 0:TT, :]
        st_f = [f[:, :, :].rearrange("p c l -> p (c l)").bitcast(f32) for f in (f_h, f_l)]

        sc = [es.enter_context(nc.psum_tensor(f"sc{i}", [P, 2 * D], f32)) for i in range(2)]
        av = es.enter_context(nc.psum_tensor("av", [P, D], f32))
        pa = es.enter_context(nc.psum_tensor("pa", [P, D], f32))
        pc = [es.enter_context(nc.psum_tensor(f"pc{i}", [P, D], f32)) for i in range(2)]

        q_dram = nc.dram_tensor("q_scratch", [2, D, L], f16, kind="Internal").ap()
        k_dram = nc.dram_tensor("k_scratch", [2, KV, L], f16, kind="Internal").ap()

        ld_ident, ld_wq, ld_wk, ld_wv, ld_wo = sem("ld_ident"), sem("ld_wq"), sem("ld_wk"), sem("ld_wv"), sem("ld_wo")
        ld_mask, ld_small, ld_rows = sem("ld_mask"), sem("ld_small"), sem("ld_rows")
        ld_f = [sem("ld_f0"), sem("ld_f1")]
        f8_done = sem("f8_done")
        ld_x, ld_c, ld_xb = sem("ld_x"), sem("ld_c"), sem("ld_xb")
        set_ready, set_high, set_free = sem("set_ready"), sem("set_high"), sem("set_free")
        sm_rows, masks_f, consts_dve, consts_pool, tanh_g = sem("sm_rows"), sem("masks_f"), sem("consts_dve"), sem("consts_pool"), sem("tanh_g")
        a_ready, a_high, a_free = sem("a_ready"), sem("a_high"), sem("a_free")
        c_ready, c_free = sem("c_ready"), sem("c_free")
        stats = [sem("stats1"), sem("stats2")]
        bnagg = [sem("bnagg1"), sem("bnagg2")]
        vareps = [sem("vareps1"), sem("vareps2")]
        rstd = [sem("rstd1"), sem("rstd2")]
        shift = [sem("shift1"), sem("shift2")]
        normed = [sem("normed1"), sem("normed2")]
        q_out, qs_in, k_out, ks_in = sem("q_out"), sem("qs_in"), sem("k_out"), sem("ks_in")
        mq_ready, mq_sum, padc_ready = sem("mq_ready"), sem("mq_sum"), sem("padc_ready")
        m_ready, m_free, t_ready, t_free = sem("m_ready"), sem("m_free"), sem("t_ready"), sem("t_free")
        exp_done, av_ready, un_ready = sem("exp_done"), sem("av_ready"), sem("un_ready")
        mr_ready, mr_high, mr_free, mr_in = sem("mr_ready"), sem("mr_high"), sem("mr_free"), sem("mr_in")
        den_in, att_in = sem("den_in"), [sem("att_in0"), sem("att_in1")]
        recip_done, rd_high, rd_ready = sem("recip_done"), sem("rd_high"), sem("rd_ready")
        at_high, at_ready = sem("at_high"), sem("at_ready")
        xb_ready = sem("xb_ready")
        x2_high = sem("x2_high")
        tanh_done, ga_done, ff_high, fl_ready = sem("tanh_done"), sem("ga_done"), sem("ff_high"), sem("fl_ready")
        y_ready, stored = sem("y_ready"), [sem("stored0"), sem("stored1")]
        sp_passed, pool_passed, dve_passed, pe_passed = (sem(n) for n in ("sp_passed", "pool_passed", "dve_passed",
                                                                          "pe_passed"))

        mask_qk, mask_pad = mask_qk.bitcast(u8), mask_pad.bitcast(u8)
        x_v = x.rearrange("b (t p) f -> b p t f", p=P)
        c_v = ctx.rearrange("b (t p) f -> b p t f", p=P)
        o_v = out.rearrange("b (t p) f -> b t p f", p=P)
        slabs = ([(gate_w[k * P:(k + 1) * P, :], wg8[:, k, :]) for k in range(KT)]
                 + [(up_w[k * P:(k + 1) * P, :], wu8[:, k, :]) for k in range(KT)]
                 + [(down_w[3 * k * P:3 * (k + 1) * P, :].rearrange("(c p) n -> p c n", p=P),
                     wd8[:, 3 * k:3 * k + 3, :]) for k in range(KT)])

        def iterations(eng, steps):
            for r in (-2, -1, 0, 1):
                steps(r, r % 2)
            with eng.Fori(1, 3) as j:
                for odd in (0, 1):
                    steps(2 * j + odd, odd)
            for r in (6, 7, 8, 9):
                steps(r, r % 2)

        def pieces(r, step):
            for name, n in PIECES[step]:
                if name == "mrow":
                    off = 0 if n == 1 else 1
                else:
                    off = OFF[name]
                if there(r, off):
                    yield name, n, r + off

        def m_unit(r, step):
            u, k = step // 4, step % 4
            if k > 1:
                return None
            off, g = (0, 5 + u) if u < 3 else (1, u - 3)
            return (off, g, k) if there(r, off) else None

        block = es.enter_context(nc.Block())

        @block.sync
        def _(sp):
            def passed(s, n):
                past(sp, s, n)
                if not isinstance(n, int):
                    sp.sem_inc(sp_passed, 1)

            sp.dma_start(xin[:, :, :], x_v[0]).then_inc(ld_x, 16)
            sp.dma_start(ident[:, :], ident_in).then_inc(ld_ident, 16)
            sp.dma_start(st_q[:, :, :], Wq.rearrange("(t p) i -> p t i", p=P)).then_inc(ld_wq, 16)
            sp.dma_start(cin[:, :, :], c_v[0]).then_inc(ld_c, 16)
            sp.dma_start(st_k[:, :], Wk).then_inc(ld_wk, 16)
            sp.dma_start(st_v[:, :], Wv).then_inc(ld_wv, 16)
            sp.dma_start(mask_u8[:, :, :], mask_qk.rearrange("(t p) k -> p t k", p=P)).then_inc(ld_mask, 16)
            sp.dma_start(padc_u8[:, :], mask_pad.rearrange("b (t p) -> (b t) p", p=P)).then_inc(ld_mask, 16)
            sp.dma_start(rows_in[row_bq:row_bk, :], bq.rearrange("(t p) -> t p", p=P)).then_inc(ld_mask, 16)
            sp.dma_start(rows_in[row_bk:row_gs, :], bk.rearrange("(t p) -> t p", p=P)).then_inc(ld_mask, 16)
            sp.dma_start(rows_in[row_gs:row_us, :], gate_s.rearrange("(t p) -> t p", p=P)).then_inc(ld_mask, 16)
            sp.dma_start(rows_in[row_us:row_us + FT, :], up_s.rearrange("(t p) -> t p", p=P)).then_inc(ld_mask, 16)
            sp.dma_start(bv_b[:, :], bv.partition_broadcast(P)).then_inc(ld_small, 16)
            sp.dma_start(tg[:, 0:1], g_att.partition_broadcast(P)).then_inc(ld_small, 16)
            sp.dma_start(tg[:, 1:2], g_ffn.partition_broadcast(P)).then_inc(ld_small, 16)
            sp.dma_start(spread[:, :, :], spread_in).then_inc(ld_small, 16)
            sp.dma_start(tgbo[:, :], bo.partition_broadcast(P)).then_inc(ld_small, 16)
            sp.dma_start(dsb[:, :], down_s.partition_broadcast(P)).then_inc(ld_small, 16)
            sp.dma_start(padr_u8[:, :, :], mask_pad.partition_broadcast(P)).then_inc(ld_rows, 16)
            for s in range(2):
                sp.dma_start(st_f[s][:, :], slabs[s][0]).then_inc(ld_f[s], 16)
            sp.wait_ge(set_ready, 4)
            sp.dma_start(st_q[:, :, :], Wo.rearrange("(t p) i -> p t i", p=P)).then_inc(ld_wo, 16)

            for t in range(TT):
                sp.sem_inc(stored[t], 16)

            def slab(s):
                sp.wait_ge(f8_done, s - 1)
                dst = st_f[s % 2][:, :]
                if s >= 2 * KT:
                    dst = dst.rearrange("p (c n) -> p c n", c=3)
                sp.dma_start(dst, slabs[s][0]).then_inc(ld_f[s % 2], 16)

            def steps(r, par):
                for step in range(STEPS):
                    if step == 0 and there(r, 2) and not (isinstance(r, int) and r == -2):
                        passed(normed[0], 2 * (r + 2))
                        sp.dma_start(xin[:, :, :], x_v[r + 2]).then_inc(ld_x, 16)
                    if step == 0 and there(r, -1):
                        passed(un_ready, 8 * r)
                        passed(recip_done, r - 1)
                        for j in range(HPG):
                            sp.dma_start(den[G * j:G * j + G, :],
                                         un[32 * j + HD:32 * j + HD + 1, :, :]).then_inc(den_in, 16)
                        gather(r - 1, 1)
                    if step == 1 and there(r, 1):
                        b = r + 1
                        passed(q_out, 32 * (b + 1))
                        passed(t_ready, 16 * r)
                        for hf in range(2):
                            for s in range(3):
                                src = q_dram[(0, 1, 0)[s]].rearrange("(p f d) n -> f d p n", f=2, d=HD)[hf]
                                sp.dma_start(qs[1 - par][64 * hf + HD * s:64 * hf + HD * (s + 1), :, :],
                                             src).then_inc(qs_in, 16)
                    if step == 2 and there(r, 2) and not (isinstance(r, int) and r == -2):
                        passed(a_ready, 7 * (r + 1) + 6)
                        sp.dma_start(cin[:, :, :], c_v[r + 2]).then_inc(ld_c, 16)
                    if step == 3 and there(r, 1):
                        b = r + 1
                        passed(a_free, 7 * b + 7)
                        passed(ks_in, 96 * b)
                        sp.dma_start(k_dram[0], kh[:, :]).then_inc(k_out, 16)
                        sp.dma_start(k_dram[1], kl[:, :]).then_inc(k_out, 16)
                        passed(k_out, 32 * (b + 1))
                        if isinstance(b, int) and b < 2:
                            sp.wait_ge(sm_rows, 1)
                        for hf in range(2):
                            for s in range(3):
                                src = k_dram[(0, 0, 1)[s]].rearrange("(g d) n -> d g n", d=HD)
                                sp.dma_start(ks[1 - par][64 * hf + HD * s:64 * hf + HD * (s + 1), :, :],
                                             src).then_inc(ks_in, 16)
                    if step in (4, 8) and there(r, -2):
                        t = step // 4 - 1
                        passed(y_ready, 2 * (r - 2) + t + 1)
                        sp.dma_start(o_v[r - 2][t], yt[:, t, :]).then_inc(stored[t], 16)
                    if step in (14, 30) and there(r, 0 if step == 14 else 1):
                        half, b = (1, r) if step == 14 else (0, r + 1)
                        p_ = par if step == 14 else 1 - par
                        passed(mr_free, 2 * b + half + 1)
                        for v, rows in ((0, nm_h), (1, nm_l)):
                            for hf in range(2):
                                row = 64 * hf + 3 * HD + v
                                sp.dma_start(qs[p_][row:row + 1, 8 * half:8 * half + 8, :],
                                             rows[8 * hf:8 * hf + 8, :]).then_inc(mr_in, 16)
                    if step == 16 and there(r, 2):
                        b = r + 2
                        passed(a_free, 7 * b + 4)
                        passed(qs_in, 96 * b)
                        sp.dma_start(q_dram[0].rearrange("(t p) n -> p t n", p=P), qh[:, :, :]).then_inc(q_out, 16)
                        sp.dma_start(q_dram[1].rearrange("(t p) n -> p t n", p=P), ql[:, :, :]).then_inc(q_out, 16)
                    if step == 16 and there(r, 0):
                        passed(c_free, C_USES * (r - 1) + 4)
                        sp.dma_start(xb[:, :, :], x_v[r]).then_inc(ld_xb, 16)
                    if step == 17 and there(r, 0):
                        passed(un_ready, 8 * r + 4)
                        gather(r, 0)
                    if isinstance(r, int) and (r == -1 or r == 0 and step < 16) and step % 4 == 3:
                        slab(2 + (step // 4 if r == -1 else 8 + step // 4)) if (r == 0 or step // 4 < 8) and \
                            2 + (step // 4 if r == -1 else 8 + step // 4) < len(slabs) else None
                if isinstance(r, int) and r == 9:
                    for t in range(TT):
                        sp.wait_ge(stored[t], 16 * (NB + 1))

            def gather(b, half):
                passed(c_free, C_USES * (b - 1) + 2)
                for gp in range(2):
                    for j in range(HPG):
                        at = 64 * gp + HD * j
                        sp.dma_start(att_u[at:at + HD, 2 * half:2 * half + 2, :],
                                     un[32 * j:32 * j + HD, 4 * half + gp:4 * half + 4:2, :]).then_inc(att_in[half], 16)

            iterations(sp, steps)

        @block.gpsimd
        def _(pool):
            def passed(s, n):
                past(pool, s, n)
                if not isinstance(n, int):
                    pool.sem_inc(pool_passed, 1)

            pool.memset(mhalf[:, :], -0.5)
            for i in range(2):
                last = pool.memset(va[i][:, :, :, HD:32], 1.0)
            last.then_inc(consts_pool, 1)
            pool.wait_ge(consts_pool, 1)

            def power(which, count):
                passed(vareps[which], count)
                pool.tensor_tensor(rs[which][:, :], ve[which][:, :], mhalf[:, :], ALU.pow).then_inc(rstd[which], 1)

            def pad_row(b, p_):
                if isinstance(b, int) and b == 0:
                    pool.wait_ge(ld_rows, 16)
                    pool.wait_ge(masks_f, 4)
                passed(m_ready, 16 * (b - 1))
                pool.tensor_copy(padrow[:, :], padr_u8[:, b, :]).then_inc(mq_sum, 1)
                passed(mq_sum, 2 * b + 1)
                pool.tensor_scalar(padrow[:, :], padrow[:, :], -BIG, None, ALU.mult).then_inc(mq_sum, 1)
                passed(mq_sum, 2 * b + 2)
                passed(m_free, 16 * (b - 1))
                for t in range(TT):
                    pool.tensor_tensor(mq[p_][:, t, :], mask_q[:, t, :], padrow[:, :], ALU.add).then_inc(mq_ready, 1)

            def steps(r, par):
                for step in range(STEPS):
                    if step == 0 and there(r, -2):
                        split_low(r - 2, 11)
                    if step == 2 and there(r, 1):
                        passed(mq_ready, 2 * (r + 1)) if not isinstance(r, int) or r >= 0 else None
                        pad_row(r + 1, 1 - par)
                    if step in (3, 7) and there(r, -2):
                        t = step // 4
                        passed(c_free, C_USES * (r - 2) + 19 + t)
                        pool.tensor_tensor(yt[:, t, :], yt[:, t, :], x2[:, t, :], ALU.add).then_inc(y_ready, 1)
                    if step == 5 and there(r, 2):
                        power(0, r + 3)
                    if step == 12 and there(r, 0):
                        pass
                    if step == 13 and there(r, -1):
                        power(1, r)
                    if step == 19 and there(r, 0):
                        if isinstance(r, int) and r == 0:
                            pool.wait_ge(consts_dve, 1)
                        passed(ld_xb, 16 * (r + 1))
                        for t in range(TT):
                            last = pool.tensor_tensor(xb[:, t, :], xb[:, t, :], tgbo[:, :], ALU.add)
                        last.then_inc(xb_ready, 1)
                    if step == 30 and there(r, 1):
                        if isinstance(r, int) and r == -1:
                            pool.wait_ge(consts_dve, 2)
                        passed(t_free, 16 * r)
                        pool.tensor_copy(padc[1 - par][:, :],
                                         padc_all[:, 2 * (r + 1):2 * (r + 1) + 2] if isinstance(r, int) else
                                         padc_all[:, bass.ds(2 * (r + 1), 2)]).then_inc(padc_ready, 1)
                    for name, n, b in pieces(r, step):
                        if name == "fsplit":
                            split_low(b, n)

            def split_low(b, c):
                passed(ff_high, FT * b + c + 1)
                if c == 0:
                    passed(c_ready, C_USES * b)
                pool.tensor_tensor(f_l[:, c, :], ff[:, c % 4, :], f_h[:, c, :], ALU.subtract).then_inc(fl_ready, 1)

            iterations(pool, steps)

        @block.scalar
        def _(act):
            def high(dst, src, scale, s, n):
                act.wait_ge(set_ready, n)
                act.activation(dst, src, ACT.Copy, scale=scale).then_inc(s, 1)

            act.wait_ge(ld_small, 96)
            act.activation(tg[:, :], tg[:, :], ACT.Tanh).then_inc(tanh_g, 1)

            def set_up(lo, hi):
                for n in range(lo, hi):
                    bank = sc[n % 4 // 2][:, D * (n % 2):D * (n % 2) + D]
                    if n < 4:
                        high(wq_h[:, n, :], bank, SWQK, set_high, n + 1)
                    elif n == 4:
                        high(wk_h[:, :, :], bank, SWQK, set_high, n + 1)
                    elif n == 5:
                        high(wv_h[:, :, :], bank, SWVO, set_high, n + 1)
                    elif n >= 8:
                        high(wo_h[:, n - 8, :], bank, SWVO, set_high, n + 1)

            def to_f8(s):
                act.wait_ge(ld_f[s % 2], 16 * (s // 2 + 1))
                src = st_f[s % 2][:, :]
                if s >= 2 * KT:
                    src = src.rearrange("p (c n) -> p c n", c=3)
                act.activation(slabs[s][1], src, ACT.Copy, saturate=False).then_inc(f8_done, 1)

            def steps(r, par):
                if isinstance(r, int) and r == -2:
                    set_up(0, SETUP_USES)
                for step in range(STEPS):
                    u = step // 4
                    if step == 0 and there(r, -2):
                        split_high(r - 2, 11)
                    if step == 0 and there(r, -1):
                        sums(r - 1, 7)
                    if step % 4 == 0 and u and there(r, 0):
                        sums(r, u - 1)
                    if step % 4 > 1 and there(r, 0):
                        n = 16 * r + 2 * u + step % 4 - 1
                        act.wait_ge(t_free, n)
                        unit = 2 * (u % 2) + step % 4 - 2
                        act.activation(ws[:, unit, :, :], ws[:, unit, :, :], ACT.Exp, scale=1.0 / SSC).then_inc(exp_done, 1)
                    for name, n, b in pieces(r, step):
                        if name == "norm1":
                            past(act, shift[0], b + 1)
                            past(act, a_ready, 7 * (b - 1) + 2)
                            for t in range(TT):
                                act.activation(xn[:, t, :], xin[:, t, :], ACT.Identity, bias=nb_[0][:, t:t + 1],
                                               scale=rs[0][:, t:t + 1]).then_inc(normed[0], 1)
                        if name == "norm2":
                            past(act, shift[1], b + 1)
                            past(act, c_ready, C_USES * (b - 1) + 6)
                            for t in range(TT):
                                act.activation(x2n[:, t, :], x2[:, t, :], ACT.Identity, bias=nb_[1][:, t:t + 1],
                                               scale=rs[1][:, t:t + 1]).then_inc(normed[1], 1)
                        if name == "xT":
                            act.wait_ge(a_ready, 7 * b + n + 1)
                            act.activation(xh[:, 2 * n:2 * n + 2, :], pa[:, :].rearrange("p (k l) -> p k l", k=2), ACT.Copy).then_inc(a_high, 1)
                        if name == "q":
                            if isinstance(b, int) and b == 0:
                                act.wait_ge(set_free, 8)
                            act.wait_ge(a_ready, 7 * b + n + 3)
                            past(act, q_out, 32 * b)
                            act.activation(qh[:, 2 * n, :], pa[:, 0:L], ACT.Identity, bias=bq_c[:, 2 * n:2 * n + 1])
                            act.activation(qh[:, 2 * n + 1, :], pa[:, L:2 * L], ACT.Identity,
                                           bias=bq_c[:, 2 * n + 1:2 * n + 2]).then_inc(a_high, 1)
                        if name == "cT":
                            act.wait_ge(a_ready, 7 * b + n + 5)
                            act.activation(ch[:, 2 * n:2 * n + 2, :], pa[:, :].rearrange("p (k l) -> p k l", k=2), ACT.Copy,
                                           scale=SX).then_inc(a_high, 1)
                        if name == "kv":
                            act.wait_ge(a_ready, 7 * b + 7)
                            past(act, k_out, 32 * b)
                            act.activation(kh[:, :], pa[:, 0:L], ACT.Identity, bias=bk_c[:, :]).then_inc(a_high, 1)
                        if name == "mrow":
                            act.wait_ge(mr_ready, 2 * b + n + 1)
                            past(act, mr_in, 64 * (2 * b + n))
                            act.activation(nm_h[:, :], av[0:H // 2, 0:L], ACT.Copy, scale=-1.0 / SM).then_inc(mr_high, 1)
                        if name == "split_att":
                            act.wait_ge(c_free, C_USES * b + n + 1)
                            past(act, c_ready, C_USES * (b - 1) + 4)
                            act.activation(at_h[:, 2 * n:2 * n + 2, :], att[:, 2 * n:2 * n + 2, :], ACT.Copy).then_inc(at_high, 1)
                        if name == "x2T":
                            act.wait_ge(c_ready, C_USES * b + n + 5)
                            act.activation(h2_h[:, 2 * n:2 * n + 2, :], pc[n][:, :].rearrange("p (k l) -> p k l", k=2), ACT.Copy).then_inc(x2_high, 1)
                        if name == "gu":
                            act.wait_ge(c_ready, C_USES * b + n + 7)
                            past(act, ga_done, FT * b + n - 1)
                            act.activation(th[:, n % 2, :], pc[n % 2][:, 0:L], ACT.Tanh, scale=tanh_s[:, n:n + 1]).then_inc(tanh_done, 1)
                        if name == "fsplit":
                            split_high(b, n)
                    if isinstance(r, int) and (r == -1 or r == 0 and step < 16) and step % 4 == 3:
                        s = step // 4 + (0 if r == -1 else 8)
                        if s < len(slabs):
                            to_f8(s)

            def split_high(b, c):
                act.wait_ge(c_free, C_USES * b + c + 7)
                if c == 0:
                    past(act, c_ready, C_USES * b)
                act.activation(f_h[:, c, :], ff[:, c % 4, :], ACT.Copy).then_inc(ff_high, 1)

            def sums(b, g):
                act.wait_ge(av_ready, 8 * b + g + 1)
                past(act, att_in[g // 4], 128 * b)
                past(act, den_in, 64 * b)
                act.activation(un[:, g, :], av[:, 0:L], ACT.Copy).then_inc(un_ready, 1)

            iterations(act, steps)

        @block.vector
        def _(dve):
            def passed(s, n):
                past(dve, s, n)
                if not isinstance(n, int):
                    dve.sem_inc(dve_passed, 1)

            for i in range(2):
                for hf in range(2):
                    last = dve.memset(ks[i][64 * hf + 32:64 * hf + 64, :, :], SM)
            last.then_inc(sm_rows, 1)
            dve.wait_ge(ld_mask, 96)
            dve.tensor_copy(mask_f[:, :, :], mask_u8[:, :, :]).then_inc(masks_f, 1)
            dve.tensor_copy(rows_in[0:NB * TT, :], padc_u8[:, :]).then_inc(masks_f, 1)
            dve.wait_ge(masks_f, 1)
            dve.tensor_scalar(mask_q[:, :, :], mask_f[:, :, :], -BIG, None, ALU.mult).then_inc(masks_f, 2)
            dve.wait_ge(tanh_g, 1)
            dve.tensor_scalar(tgbo[:, :], tgbo[:, :], tg[:, 0:1], None, ALU.mult)
            dve.tensor_scalar(tgo[:, :], tg[:, 0:1], 1.0 / (SWVO * SA), None, ALU.mult)
            dve.tensor_scalar(dsb[:, :], dsb[:, :], tg[:, 1:2], 1.0 / SF, ALU.mult, ALU.mult).then_inc(consts_dve, 1)

            def set_up():
                for n in range(SETUP_USES):
                    bank = sc[n % 4 // 2][:, D * (n % 2):D * (n % 2) + D]
                    if n == 6:
                        dve.wait_ge(set_ready, n + 1)
                        dve.tensor_scalar(mask_k[:, :, :], bank.rearrange("p (t l) -> p t l", t=TT), -BIG, None, ALU.mult).then_inc(set_free, 1)
                        continue
                    if n == 7:
                        dve.wait_ge(set_ready, n + 1)
                        dve.tensor_scalar(padc_all[:, :], bank[:, 0:row_bq], -BIG, None, ALU.mult)
                        dve.tensor_scalar(bq_c[:, :], bank[:, row_bq:row_bk], SQK, None, ALU.mult)
                        dve.tensor_scalar(bk_c[:, :], bank[:, row_bk:row_gs], SQK, None, ALU.mult)
                        dve.tensor_scalar(tanh_s[:, :], bank[:, row_gs:row_us], 0.5 / SX, None, ALU.mult)
                        dve.tensor_scalar(gs_c[:, :], bank[:, row_gs:row_us], 0.5 * SF / (SX * SX), None,
                                          ALU.mult).then_inc(consts_dve, 1)
                        dve.wait_ge(consts_dve, 2)
                        dve.tensor_tensor(fuse_s[:, :], bank[:, row_us:row_us + FT], gs_c[:, :],
                                          ALU.mult).then_inc(set_free, 1)
                        continue
                    w_h, w_l, scale = ((wq_h[:, n, :], wq_l[:, n, :], SWQK) if n < 4 else
                                       (wk_h[:, :, :], wk_l[:, :, :], SWQK) if n == 4 else
                                       (wv_h[:, :, :], wv_l[:, :, :], SWVO) if n == 5 else
                                       (wo_h[:, n - 8, :], wo_l[:, n - 8, :], SWVO))
                    dve.wait_ge(set_high, n + 1 if n < 6 else n - 1)
                    dve.scalar_tensor_tensor(out=w_l, in0=bank, scalar=scale, in1=w_h, op0=ALU.mult,
                                             op1=ALU.subtract).then_inc(set_free, 1)

            def tile_stats(which, b, t, src):
                dve.bn_stats(bst[which][:, t, :], src[:, t, :]).then_inc(stats[which], 1)

            def piece(name, n, b, par):
                if name == "stats1":
                    past(dve, ld_x, 16 * (b + 1))
                    for t in range(TT):
                        tile_stats(0, b, t, xin)
                    variance(0, b)
                if name == "stats2":
                    pass
                if name in ("shift1", "shift2"):
                    i = int(name[-1]) - 1
                    dve.wait_ge(rstd[i], b + 1)
                    dve.scalar_tensor_tensor(out=nb_[i][:, :], in0=mv[i][:, :, 0], scalar=-1.0, in1=rs[i][:, :],
                                             op0=ALU.mult, op1=ALU.mult).then_inc(shift[i], 1)
                if name == "xT":
                    dve.wait_ge(a_high, 7 * b + n + 1)
                    dve.tensor_tensor(xl[:, 2 * n:2 * n + 2, :], pa[:, :].rearrange("p (k l) -> p k l", k=2),
                                      xh[:, 2 * n:2 * n + 2, :], ALU.subtract).then_inc(a_free, 1)
                if name == "q":
                    dve.wait_ge(a_high, 7 * b + n + 3)
                    dve.scalar_tensor_tensor(out=ql[:, 2 * n, :], in0=pa[:, 0:L], scalar=bq_c[:, 2 * n:2 * n + 1],
                                             in1=qh[:, 2 * n, :], op0=ALU.add, op1=ALU.subtract)
                    dve.scalar_tensor_tensor(out=ql[:, 2 * n + 1, :], in0=pa[:, L:2 * L], scalar=bq_c[:, 2 * n + 1:2 * n + 2],
                                             in1=qh[:, 2 * n + 1, :], op0=ALU.add, op1=ALU.subtract).then_inc(a_free, 1)
                if name == "cT":
                    dve.wait_ge(a_high, 7 * b + n + 5)
                    dve.scalar_tensor_tensor(out=cl[:, 2 * n:2 * n + 2, :], in0=pa[:, :].rearrange("p (k l) -> p k l", k=2),
                                             scalar=SX, in1=ch[:, 2 * n:2 * n + 2, :], op0=ALU.mult,
                                             op1=ALU.subtract).then_inc(a_free, 1)
                if name == "kv":
                    dve.wait_ge(a_high, 7 * b + 7)
                    dve.scalar_tensor_tensor(out=kl[:, :], in0=pa[:, 0:L], scalar=bk_c[:, :], in1=kh[:, :], op0=ALU.add,
                                             op1=ALU.subtract)
                    if isinstance(b, int) and b < 2:
                        dve.wait_ge(consts_pool, 1)
                    past(dve, av_ready, 8 * (b - 1))
                    for t in range(TT):
                        last = dve.scalar_tensor_tensor(
                            out=va[par][:, t, :, 0:HD],
                            in0=pa[:, L + KV * t:L + KV * (t + 1)].rearrange("p (g d) -> p g d", d=HD),
                            scalar=1.0 / (SX * SWVO), in1=bv_b[:, :].rearrange("p (g d) -> p g d", d=HD),
                            op0=ALU.mult, op1=ALU.add)
                    last.then_inc(a_free, 1)
                if name == "mrow":
                    dve.wait_ge(mr_high, 2 * b + n + 1)
                    dve.scalar_tensor_tensor(out=nm_l[:, :], in0=av[0:H // 2, 0:L], scalar=-1.0 / SM, in1=nm_h[:, :],
                                             op0=ALU.mult, op1=ALU.subtract).then_inc(mr_free, 1)
                if name == "recip":
                    dve.wait_ge(den_in, 64 * (b + 1))
                    dve.reciprocal(rden[:, :], den[:, :]).then_inc(recip_done, 1)
                    dve.wait_ge(recip_done, b + 1)
                    past(dve, c_ready, C_USES * (b - 1) + 2)
                    dve.tensor_scalar(rd[0:H, :], rden[:, :], SA, None, ALU.mult).then_inc(rd_high, 1)
                    dve.wait_ge(rd_high, b + 1)
                    dve.scalar_tensor_tensor(out=rd[H:2 * H, :], in0=rden[:, :], scalar=SA, in1=rd[0:H, :], op0=ALU.mult,
                                             op1=ALU.subtract).then_inc(rd_ready, 1)
                if name == "spread":
                    dve.wait_ge(c_ready, C_USES * b + n + 1)
                    dve.wait_ge(att_in[n], 128 * (b + 1))
                    dve.tensor_tensor(att[:, 2 * n:2 * n + 2, :], pc[n][:, :].rearrange("p (k l) -> p k l", k=2),
                                      att_u[:, 2 * n:2 * n + 2, :], ALU.mult).then_inc(c_free, 1)
                if name == "split_att":
                    dve.wait_ge(at_high, 2 * b + n + 1)
                    dve.tensor_tensor(at_l[:, 2 * n:2 * n + 2, :], att[:, 2 * n:2 * n + 2, :], at_h[:, 2 * n:2 * n + 2, :],
                                      ALU.subtract).then_inc(at_ready, 1)
                if name == "out":
                    dve.wait_ge(c_ready, C_USES * b + n + 3)
                    dve.wait_ge(xb_ready, b + 1)
                    past(dve, y_ready, 2 * b)
                    dve.scalar_tensor_tensor(out=x2[:, n, :], in0=pc[n][:, :], scalar=tgo[:, :], in1=xb[:, n, :],
                                             op0=ALU.mult, op1=ALU.add).then_inc(c_free, 1)
                    dve.wait_ge(c_free, C_USES * b + n + 3)
                    tile_stats(1, b, n, x2)
                    if n == 1:
                        variance(1, b)
                if name == "x2T":
                    dve.wait_ge(x2_high, 2 * b + n + 1)
                    dve.tensor_tensor(h2_l[:, 2 * n:2 * n + 2, :], pc[n][:, :].rearrange("p (k l) -> p k l", k=2),
                                      h2_h[:, 2 * n:2 * n + 2, :], ALU.subtract).then_inc(c_free, 1)
                if name == "gu":
                    past(dve, c_free, C_USES * b + n + 6)
                    dve.wait_ge(tanh_done, FT * b + n + 1)
                    dve.scalar_tensor_tensor(out=ga[:, :], in0=th[:, n % 2, :], scalar=1.0, in1=pc[n % 2][:, 0:L],
                                             op0=ALU.add, op1=ALU.mult).then_inc(ga_done, 1)
                    dve.wait_ge(ga_done, FT * b + n + 1)
                    past(dve, fl_ready, FT * b + n - 3)
                    dve.scalar_tensor_tensor(out=ff[:, n % 4, :], in0=pc[n % 2][:, L:2 * L], scalar=fuse_s[:, n:n + 1],
                                             in1=ga[:, :], op0=ALU.mult, op1=ALU.mult).then_inc(c_free, 1)
                if name == "down_b":
                    dve.wait_ge(c_ready, C_USES * b + n + 19)
                    dve.wait_ge(stored[n], 16 * (b + 1))
                    dve.tensor_tensor(yt[:, n, :], pc[n][:, :], dsb[:, :], ALU.mult).then_inc(c_free, 1)

            def variance(which, b):
                passed(stats[which], 2 * (b + 1))
                for t in range(TT):
                    last = dve.bn_aggr(mv[which][:, t, :], bst[which][:, t, :])
                last.then_inc(bnagg[which], 1)
                dve.wait_ge(bnagg[which], b + 1)
                dve.tensor_scalar(ve[which][:, :], mv[which][:, :, 1], 1e-5, 1.0 / (SX * SX), ALU.add,
                                  ALU.mult).then_inc(vareps[which], 1)

            def steps(r, par):
                if isinstance(r, int) and r == -2:
                    dve.wait_ge(ld_x, 16)
                    piece("stats1", 0, 0, 0)
                    dve.wait_ge(rstd[0], 1)
                    piece("shift1", 0, 0, 0)
                    set_up()
                for step in range(STEPS):
                    u, k = step // 4, step % 4
                    unit = m_unit(r, step)
                    if unit is not None:
                        off, g, t = unit
                        b, p_ = r + off, (par if off == 0 else 1 - par)
                        past(dve, mq_ready, 2 * (b + 1))
                        past(dve, m_free, 16 * b + 2 * g + t - 1)
                        passed(m_ready, 16 * b + 2 * g + t + 1)
                        for j in range(HPG):
                            pair, hf = 2 * g + j // 2, j % 2
                            col = 16 * (g // 4) + 8 * hf + pair % 8
                            last = dve.tensor_tensor_reduce(junk[:, HPG * t + j, :], sc[k][:, place(j)], mq[p_][:, t, :], 1.0,
                                                            -3.4e38, ALU.add, ALU.max, mx[:, t, col:col + 1])
                        last.then_inc(m_free, 1)
                    if k > 1 and there(r, 0):
                        kt = k - 2
                        past(dve, padc_ready, r + 1)
                        dve.wait_ge(t_ready, 16 * r + 2 * u + kt + 1)
                        past(dve, av_ready, 8 * r + u - 1)
                        dve.scalar_tensor_tensor(
                            out=ws[:, 2 * (u % 2) + kt, :, :], in0=sc[kt][:, :].rearrange("p (j l) -> p j l", j=HPG),
                            scalar=padc[par][:, kt:kt + 1], in1=mask_k[:, kt:kt + 1, :].broadcast_to([P, HPG, L]),
                            op0=ALU.add, op1=ALU.add).then_inc(t_free, 1)
                    before = r if step else r - 1
                    for name, n, b in pieces(before, (step - 1) % STEPS):
                        if isinstance(r, int) and r == -2 and name in ("stats1", "shift1"):
                            continue
                        piece(name, n, b, 1 - par if name == "kv" else par)

            iterations(dve, steps)

        @block.tensor
        def _(pe):
            mm = pe.matmul
            THREE = lambda wh, wl, dh, dl: ((wh, dh), (wh, dl), (wl, dh))

            def set_up():
                for n in range(SETUP_USES):
                    bank = sc[n % 4 // 2][:, D * (n % 2):D * (n % 2) + D]
                    if n >= 4:
                        pe.wait_ge(set_free, n - 3)
                    if n < 4 or n >= 8:
                        if n == 0:
                            pe.wait_ge(ld_ident, 16)
                            pe.wait_ge(ld_wq, 16)
                        if n == 8:
                            pe.wait_ge(ld_wo, 16)
                        k = n % 4
                        for t in range(KT):
                            last = pe.transpose(bank[:, t * P:(t + 1) * P], st_q[:, t, k * P:(k + 1) * P], ident[:, :])
                    elif n in (4, 5):
                        pe.wait_ge((ld_wk, ld_wv)[n - 4], 16)
                        st = (st_k, st_v)[n - 4]
                        for k in range(KT):
                            last = pe.transpose(bank[:, k * P:(k + 1) * P], st[:, k * P:(k + 1) * P], ident[:, :])
                    elif n == 6:
                        pe.wait_ge(masks_f, 2)
                        for kt in range(TT):
                            for t in range(TT):
                                last = pe.transpose(bank[:, kt * L + t * P:kt * L + (t + 1) * P],
                                                    mask_f[:, t, kt * P:(kt + 1) * P], ident[:, :])
                    else:
                        last = pe.transpose(bank[:, 0:row_us + FT], rows_in[:, :], ident[0:row_us + FT, 0:row_us + FT])
                    last.then_inc(set_ready, 1)

            def a_bank(b, use):
                past(pe, a_free, A_USES * b + use)

            def c_bank(b, use):
                past(pe, c_free, C_USES * b + use - 1)
                return pc[use % 2]

            def maxima(b, g, t, p_, k):
                if g == 0 and t == 0:
                    pe.wait_ge(qs_in, 96 * (b + 1))
                    pe.wait_ge(ks_in, 96 * (b + 1))
                    if isinstance(b, int) and b == 0:
                        pe.wait_ge(set_free, SETUP_USES)
                past(pe, m_free, 16 * b + 2 * g - 1 + t)
                past(pe, t_free, 16 * (b - 1) + 2 * (g + 2) + t + 1 if g < 6 else 16 * b + 2 * (g - 6) + t + 1)
                for j in range(HPG):
                    pair, at = 2 * g + j // 2, 64 * (j % 2)
                    last = mm(sc[k][:, place(j)], qs[p_][at:at + 3 * HD, pair, t * P:(t + 1) * P],
                              ks[p_][at:at + 3 * HD, g, :], start=True, stop=True)
                last.then_inc(m_ready, 1)

            def scores(b, g, kt, p_):
                if g in (0, 4) and kt == 0:
                    pe.wait_ge(mr_in, 64 * (2 * b + g // 4 + 1))
                past(pe, t_free, 16 * b + 2 * g + kt - 1)
                done = 16 * b + 2 * (g + 5) + kt + 1
                past(pe, m_free, min(done, 16 * NB) if isinstance(done, int) else done)
                for j in range(HPG):
                    pair, at = 2 * g + j // 2, 64 * (j % 2)
                    last = mm(sc[kt][:, place(j)], ks[p_][at:at + 3 * HD + 2, g, kt * P:(kt + 1) * P],
                              qs[p_][at:at + 3 * HD + 2, pair, :], start=True, stop=True)
                last.then_inc(t_ready, 1)

            def weighted(b, g, p_):
                pe.wait_ge(exp_done, 16 * b + 2 * g + 2)
                past(pe, un_ready, 8 * b + g)
                rows = 2 * b + (1 if g < 3 else 2 if g < 7 else 3)
                past(pe, mr_free, min(rows, 2 * NB) if isinstance(rows, int) else rows)
                for kt in range(TT):
                    for j in range(HPG):
                        last = mm(av[32 * j:32 * (j + 1), 0:L], va[p_][:, kt, g, :],
                                  ws[:, 2 * (g % 2) + kt, 2 * (j % 2) + j // 2, :],
                                  start=kt == 0, stop=kt == TT - 1)
                last.then_inc(av_ready, 1)

            def piece(name, n, b):
                if name == "xT":
                    if n == 0:
                        pe.wait_ge(normed[0], 2 * (b + 1))
                    a_bank(b, n)
                    for i in range(2):
                        for t in range(TT):
                            last = pe.transpose(pa[:, L * i + P * t:L * i + P * (t + 1)],
                                                xn[:, t, (2 * n + i) * P:(2 * n + i + 1) * P], ident[:, :])
                    last.then_inc(a_ready, 1)
                if name == "q":
                    a_bank(b, 2 + n)
                    for i in range(2):
                        cols = slice((2 * n + i) * P, (2 * n + i + 1) * P)
                        for k in range(KT):
                            for s, (w, d) in enumerate(THREE(wq_h, wq_l, xh, xl)):
                                last = mm(pa[:, L * i:L * (i + 1)], w[:, k, cols], d[:, k, :], start=k == 0 and s == 0,
                                          stop=k == KT - 1 and s == 2)
                    last.then_inc(a_ready, 1)
                if name == "cT":
                    if n == 0:
                        pe.wait_ge(ld_c, 16 * (b + 1))
                    a_bank(b, 4 + n)
                    for i in range(2):
                        for t in range(TT):
                            last = pe.transpose(pa[:, L * i + P * t:L * i + P * (t + 1)],
                                                cin[:, t, (2 * n + i) * P:(2 * n + i + 1) * P], ident[:, :])
                    last.then_inc(a_ready, 1)
                if name == "kv":
                    a_bank(b, 6)
                    for k in range(KT):
                        for s, (w, d) in enumerate(THREE(wk_h, wk_l, ch, cl)):
                            mm(pa[:, 0:L], w[:, k, :], d[:, k, :], start=k == 0 and s == 0, stop=k == KT - 1 and s == 2)
                    for t in range(TT):
                        for k in range(KT):
                            for s, (w, d) in enumerate(THREE(wv_h, wv_l, ch, cl)):
                                last = mm(pa[:, L + KV * t:L + KV * (t + 1)], d[:, k, t * P:(t + 1) * P], w[:, k, :],
                                          start=k == 0 and s == 0, stop=k == KT - 1 and s == 2)
                    last.then_inc(a_ready, 1)
                if name == "mrow":
                    pe.wait_ge(m_free, 16 * b + 8 * (n + 1))
                    past(pe, un_ready, 8 * b + 3 if n == 1 else 8 * (b - 1) + 7)
                    for t in range(TT):
                        last = pe.transpose(av[0:H // 2, P * t:P * (t + 1)], mx[:, t, 16 * n:16 * (n + 1)], ident[:, :])
                    last.then_inc(mr_ready, 1)
                if name == "spread":
                    if n == 0:
                        pe.wait_ge(rd_ready, b + 1)
                    bank = c_bank(b, n)
                    for i in range(2):
                        last = mm(bank[:, L * i:L * (i + 1)], spread[:, 2 * n + i, :], rd[:, :], start=True, stop=True)
                    last.then_inc(c_ready, 1)
                if name == "out":
                    if n == 0:
                        pe.wait_ge(at_ready, 2 * (b + 1))
                    bank = c_bank(b, 2 + n)
                    for k in range(KT):
                        for s, (d, w) in enumerate(((at_h, wo_h), (at_h, wo_l), (at_l, wo_h))):
                            last = mm(bank[:, :], d[:, k, n * P:(n + 1) * P], w[:, k, :], start=k == 0 and s == 0,
                                      stop=k == KT - 1 and s == 2)
                    last.then_inc(c_ready, 1)
                if name == "x2T":
                    if n == 0:
                        pe.wait_ge(normed[1], 2 * (b + 1))
                    bank = c_bank(b, 4 + n)
                    for i in range(2):
                        for t in range(TT):
                            last = pe.transpose(bank[:, L * i + P * t:L * i + P * (t + 1)],
                                                x2n[:, t, (2 * n + i) * P:(2 * n + i + 1) * P], ident[:, :])
                    last.then_inc(c_ready, 1)
                if name == "gu":
                    if n == 0 and isinstance(b, int) and b == 0:
                        pe.wait_ge(f8_done, len(slabs))
                    if n == 0:
                        pe.wait_ge(c_free, C_USES * b + 6)
                    bank = c_bank(b, 6 + n)
                    if not isinstance(b, int):
                        pe.sem_inc(pe_passed, 1)
                    for i, w in enumerate((wg8, wu8)):
                        for k in range(KT):
                            for s, d in enumerate((h2_h, h2_l)):
                                last = mm(bank[:, L * i:L * (i + 1)], w[:, k, n * P:(n + 1) * P], d[:, k, :],
                                          start=k == 0 and s == 0, stop=k == KT - 1 and s == 1)
                    last.then_inc(c_ready, 1)
                if name in ("down_a", "down_b"):
                    half = name == "down_b"
                    if not half:
                        c_bank(b, 18 + n)
                    if n == 0:
                        pe.wait_ge(fl_ready, FT * b + (FT if half else FT // 2))
                    if not isinstance(b, int):
                        pe.sem_inc(pe_passed, 1)
                    for c in range(FT // 2 * half, FT // 2 * (half + 1)):
                        for s, d in enumerate((f_h, f_l)):
                            last = mm(pc[n][:, :], d[:, c, n * P:(n + 1) * P], wd8[:, c, :], start=c == 0 and s == 0,
                                      stop=c == FT - 1 and s == 1)
                    if half:
                        last.then_inc(c_ready, 1)

            def steps(r, par):
                if isinstance(r, int) and r == -2:
                    set_up()
                for step in range(STEPS):
                    u, k = step // 4, step % 4
                    if step == 0 and there(r, -1):
                        weighted(r - 1, 7, 1 - par)
                    if k == 0 and u and there(r, 0):
                        weighted(r, u - 1, par)
                    unit = m_unit(r, step)
                    if unit is not None:
                        off, g, t = unit
                        maxima(r + off, g, t, par if off == 0 else 1 - par, k)
                    if k > 1 and there(r, 0):
                        scores(r, u, k - 2, par)
                    for name, n, b in pieces(r, step):
                        piece(name, n, b)

            iterations(pe, steps)


_INS = ["x", "ctx_2048", "mask_SxS2_bc0", "mask_BxS2_bk0", "g_xattn", "g_ffn", "L0_xattn_Wq", "L0_xattn_bq",
        "L0_xattn_Wk", "L0_xattn_bk", "L0_xattn_Wv", "L0_xattn_bv", "L0_xattn_Wo", "L0_xattn_bo", "L0_ffn_gate_w",
        "L0_ffn_up_w", "L0_ffn_down_w", "L0_ffn_gate_scale", "L0_ffn_up_scale", "L0_ffn_down_scale"]


def kernel(**inputs):
    import numpy as np
    import concourse.bacc as bacc
    from concourse.bass_utils import run_bass_kernel_spmd

    nc = bacc.Bacc("TRN2", target_bir_lowering=False, num_devices=1)
    arrays, args = {}, []
    to = np.zeros((2, H, KT, P), np.float16)
    for g in range(G):
        for j in range(HPG):
            at = 64 * (g % 2) + HD * j
            to[:, j * G + g, g // 2, at:at + HD] = 1.0
    consts = {"ident": np.eye(P, dtype=np.float32), "spread": to.reshape(2 * H, KT, P)}
    for name in _INS + list(consts):
        a = np.ascontiguousarray(inputs[name] if name in inputs else consts[name])
        if a.dtype == np.bool_:
            a = a.view(np.uint32)
        arrays[f"in_{name}"] = a
        args.append(nc.dram_tensor(f"in_{name}", a.shape, mybir.dt.from_np(a.dtype), kind="ExternalInput").ap())
    args.append(nc.dram_tensor("out_x", (NB, L, D), mybir.dt.float32, kind="ExternalOutput").ap())
    xattn_ffn(nc, *args)
    r = run_bass_kernel_spmd(nc, [arrays], core_ids=[0])
    return r.results[0]["out_x"]
```

```python
import concourse.bass as bass
from concourse import mybir
from contextlib import ExitStack

NB, L, D = 8, 256, 512
H, G, HD = 32, 8, 16
HPG = H // G
F = 1536
P = 128
TT = L // P
KT = D // P
FT = F // P
PAIRS = H // 2
KV = G * HD

SX = 4.0
SWQK = 16.0
SWVO = 256.0
SQK = SX * SWQK
SSC = SQK * SQK * 4.0
SM = 2048.0
SA = 64.0
SF = 64.0
BIG = 1.0e30

STEPS = 32
SUMS_AT = 2
WHEN = {
    ("load_x", 0): -64, ("stats1", 0): -62, ("power", 0): -61, ("shift1", 0): -61, ("norm1", 0): -60,
    ("xT", 0): -58, ("xT", 1): -56, ("q", 0): -44, ("q", 1): -38, ("put_q", 0): -36, ("get_q", 0): -31,
    ("load_c", 0): -62, ("cT", 0): -36, ("cT", 1): -34, ("kv", 0): -32, ("put_k", 0): -31,
    ("pad_row", 0): -30, ("padc", 0): -2,
    ("mrow", 0): -5, ("rows", 0): -4, ("mrow", 1): 11, ("rows", 1): 12,
    ("gather", 0): 19, ("den", 0): 35, ("gather", 1): 35, ("recip", 0): 39, ("load_xb", 0): 18, ("add_bo", 0): 21,
    ("spread", 0): 42, ("split_att", 0): 43, ("spread", 1): 44, ("split_att", 1): 45,
    ("out", 0): 48, ("out", 1): 50, ("power", 1): 51, ("shift2", 0): 51, ("norm2", 0): 53,
    ("x2T", 0): 54, ("x2T", 1): 56,
    **{("gu", c): 59 + 2 * c for c in range(FT)}, **{("fuse", c): 60 + 2 * c for c in range(FT)},
    **{("fsplit", c): 62 + 2 * c for c in range(FT)},
    ("down_a", 0): 83, ("down_b", 0): 85, ("down_a", 1): 87, ("down_b", 1): 89,
    ("add_y", 0): 86, ("store", 0): 87, ("add_y", 1): 90, ("store", 1): 91,
}
ROWS_AT = ((WHEN["mrow", 1] - SUMS_AT) // 4, (WHEN["mrow", 0] + STEPS - SUMS_AT) // 4)
CHAINS = {
    "a": [("xT", 0), ("xT", 1), ("q", 0), ("q", 1), ("cT", 0), ("cT", 1), ("kv", 0)],
    "b": [("spread", 0), ("spread", 1), ("out", 0), ("out", 1), ("x2T", 0), ("x2T", 1)],
    "c": [("gu", c) for c in range(FT)] + [("down", 0), ("down", 1)],
}
A_USES, B_USES, C_USES = (len(chain) for chain in CHAINS.values())
BANK = {
    **{piece: 0 for chain in "ab" for piece in CHAINS[chain]},
    **{piece: 1 + n % 2 for n, piece in enumerate(CHAINS["c"])},
}
SETUP_USES = 12
RING = 4


def bank_waits(piece, b):
    when = {**WHEN, ("down", 0): WHEN["down_a", 0], ("down", 1): WHEN["down_a", 1]}
    lines, counts = list(when), {}
    for name, chain in CHAINS.items():
        last = []
        for n, other in enumerate(chain):
            if BANK[other] == BANK[piece]:
                batches, apart = divmod(when[piece] - when[other], STEPS)
                if not apart and lines.index(other) >= lines.index(piece):
                    batches -= 1
                last.append(len(chain) * batches + n + 1)
        if last:
            count = len(chain) * b + max(last)
            counts[name] = min(count, len(chain) * NB) if isinstance(count, int) else count
    return counts


def past(eng, sem, count):
    if not isinstance(count, int) or count > 0:
        eng.wait_ge(sem, count)


def place(j):
    at = L * (2 * (j % 2) + j // 2)
    return slice(at, at + L)


def there(r, off):
    return not isinstance(r, int) or 0 <= r + off < NB


def xattn_ffn(nc, x, ctx, mask_qk, mask_pad, g_att, g_ffn, Wq, bq, Wk, bk, Wv, bv, Wo, bo,
              gate_w, up_w, down_w, gate_s, up_s, down_s, ident_in, spread_in, out):
    f32, f16, f8, u8 = mybir.dt.float32, mybir.dt.float16, mybir.dt.float8e4, mybir.dt.uint8
    ALU, ACT, AX = mybir.AluOpType, mybir.ActivationFunctionType, mybir.AxisListType
    es = ExitStack()
    with es:
        def sb(name, shape, dt):
            return es.enter_context(nc.sbuf_tensor(name, shape, dt))

        def sem(name):
            return es.enter_context(nc.semaphore(name))

        wq_h, wq_l = sb("wq_h", [P, KT, D], f16), sb("wq_l", [P, KT, D], f16)
        wo_h, wo_l = sb("wo_h", [P, KT, D], f16), sb("wo_l", [P, KT, D], f16)
        wk_h, wk_l = sb("wk_h", [P, KT, KV], f16), sb("wk_l", [P, KT, KV], f16)
        wv_h, wv_l = sb("wv_h", [P, KT, KV], f16), sb("wv_l", [P, KT, KV], f16)
        wg8, wu8, wd8 = sb("wg8", [P, KT, F], f8), sb("wu8", [P, KT, F], f8), sb("wd8", [P, FT, D], f8)
        ident, spread = sb("ident", [P, P], f32), sb("spread", [2 * H, KT, P], f16)
        bq_c, bk_c, bv_b = sb("bq_c", [P, KT], f32), sb("bk_c", [P, 1], f32), sb("bv_b", [P, KV], f32)
        tg, tgo, tgf = sb("tg", [P, 2], f32), sb("tgo", [P, 1], f32), sb("tgf", [P, 1], f32)
        tgbo, dsb = sb("tgbo", [P, D], f32), sb("dsb", [P, D], f32)
        gs_c = sb("gs_c", [P, FT], f32)
        tanh_s, fuse_s = sb("tanh_s", [P, FT], f32), sb("fuse_s", [P, FT], f32)
        mhalf = sb("mhalf", [P, 2], f32)
        mask_u8 = sb("mask_u8", [P, TT, L], u8)
        mask_q, mask_k = sb("mask_q", [P, TT, L], f32), sb("mask_k", [P, TT, L], f32)
        padr_u8 = sb("padr_u8", [P, NB, L], u8)
        padc_u8, padc_all = sb("padc_u8", [NB * TT, P], u8), sb("padc_all", [P, NB * TT], f32)
        row_bq = NB * TT
        row_bk, row_gs = row_bq + KT, row_bq + KT + 1
        row_us = row_gs + FT
        rows_in = sb("rows_in", [row_us + FT, P], f32)
        xin, xn = sb("xin", [P, TT, D], f32), sb("xn", [P, TT, D], f32)
        cin = sb("cin", [P, TT, D], f32)
        xh, xl = sb("xh", [P, KT, L], f16), sb("xl", [P, KT, L], f16)
        ch, cl = sb("ch", [P, KT, L], f16), sb("cl", [P, KT, L], f16)
        qh, ql = sb("qh", [P, KT, L], f16), sb("ql", [P, KT, L], f16)
        kh, kl = sb("kh", [P, L], f16), sb("kl", [P, L], f16)
        qs = [sb(f"qs{i}", [P, PAIRS, L], f16) for i in range(2)]
        ks = [sb(f"ks{i}", [P, G, L], f16) for i in range(2)]
        va = [sb(f"va{i}", [P, TT, G, 32], f32) for i in range(2)]
        mq = [sb(f"mq{i}", [P, TT, L], f32) for i in range(2)]
        padrow = sb("padrow", [P, L], f32)
        padc = [sb(f"padc{i}", [P, TT], f32) for i in range(2)]
        mx, junk = sb("mx", [P, TT, H], f32), sb("junk", [P, 2 * HPG, L], mybir.dt.bfloat16)
        nm_h, nm_l = sb("nm_h", [H // 2, L], f16), sb("nm_l", [H // 2, L], f16)
        ws = sb("ws", [P, 4, HPG, L], f32)
        un = sb("un", [P, G, L], f32)
        att_u, att, den, rden = sb("att_u", [P, KT, L], f32), sb("att", [P, KT, L], f32), sb("den", [H, L], f32), sb("rden", [H, L], f32)
        rd = sb("rd", [2 * H, L], f16)
        at_h, at_l = sb("at_h", [P, KT, L], f16), sb("at_l", [P, KT, L], f16)
        xb, x2n = sb("xb", [P, TT, D], f32), sb("x2n", [P, TT, D], f32)
        x2 = [sb(f"x2_{i}", [P, TT, D], f32) for i in range(2)]
        h2_h, h2_l = sb("h2_h", [P, KT, L], f16), sb("h2_l", [P, KT, L], f16)
        th, ga = sb("th", [P, RING, L], f32), sb("ga", [P, RING, L], f32)
        up, ff = sb("up", [P, RING, L], f32), sb("ff", [P, RING, L], f32)
        f_h, f_l = sb("f_h", [P, FT, L], f16), sb("f_l", [P, FT, L], f16)
        yt = sb("yt", [P, TT, D], f32)
        bst = [sb(f"bst{i}", [P, TT, 6], f32) for i in range(2)]
        mv = [sb(f"mv{i}", [P, TT, 2], f32) for i in range(2)]
        ve = [sb(f"ve{i}", [P, TT], f32) for i in range(2)]
        rs = [sb(f"rs{i}", [P, TT], f32) for i in range(2)]
        nb_ = [sb(f"nb{i}", [P, TT], f32) for i in range(2)]

        st_q = un[:, :, :].rearrange("p (t a) l -> p t (a l)", t=KT)
        st_k = att_u[:, 0:2, :].rearrange("p a l -> p (a l)")
        st_v = att_u[:, 2:4, :].rearrange("p a l -> p (a l)")
        mask_f = att[:, 0:TT, :]
        st_f = [f[:, :, :].rearrange("p c l -> p (c l)").bitcast(f32) for f in (f_h, f_l)]

        sc = [es.enter_context(nc.psum_tensor(f"sc{i}", [P, 2 * D], f32)) for i in range(2)]
        av = es.enter_context(nc.psum_tensor("av", [P, D], f32))
        work = [es.enter_context(nc.psum_tensor(f"work{i}", [P, D], f32)) for i in range(3)]

        q_dram = nc.dram_tensor("q_scratch", [2, D, L], f16, kind="Internal").ap()
        k_dram = nc.dram_tensor("k_scratch", [2, KV, L], f16, kind="Internal").ap()

        ld_ident, ld_wq, ld_wk, ld_wv, ld_wo = sem("ld_ident"), sem("ld_wq"), sem("ld_wk"), sem("ld_wv"), sem("ld_wo")
        ld_mask, ld_small, ld_rows = sem("ld_mask"), sem("ld_small"), sem("ld_rows")
        ld_f = [sem("ld_f0"), sem("ld_f1")]
        f8_done = sem("f8_done")
        ld_x, ld_c, ld_xb = sem("ld_x"), sem("ld_c"), sem("ld_xb")
        set_ready, set_high, set_free = sem("set_ready"), sem("set_high"), sem("set_free")
        sm_rows, masks_f, consts_dve, consts_pool, tanh_g = sem("sm_rows"), sem("masks_f"), sem("consts_dve"), sem("consts_pool"), sem("tanh_g")
        a_ready, a_high, a_free = sem("a_ready"), sem("a_high"), sem("a_free")
        b_ready, b_free = sem("b_ready"), sem("b_free")
        c_ready, c_free = sem("c_ready"), sem("c_free")
        stats = [sem("stats1"), sem("stats2")]
        bnagg = [sem("bnagg1"), sem("bnagg2")]
        vareps = [sem("vareps1"), sem("vareps2")]
        rstd = [sem("rstd1"), sem("rstd2")]
        shift = [sem("shift1"), sem("shift2")]
        normed = [sem("normed1"), sem("normed2")]
        q_out, qs_in, k_out, ks_in = sem("q_out"), sem("qs_in"), sem("k_out"), sem("ks_in")
        mq_ready, mq_sum, padc_ready = sem("mq_ready"), sem("mq_sum"), sem("padc_ready")
        m_ready, m_free, t_ready, t_free = sem("m_ready"), sem("m_free"), sem("t_ready"), sem("t_free")
        exp_done, av_ready, un_ready = sem("exp_done"), sem("av_ready"), sem("un_ready")
        mr_ready, mr_high, mr_free, mr_in = sem("mr_ready"), sem("mr_high"), sem("mr_free"), sem("mr_in")
        den_in, att_in = sem("den_in"), [sem("att_in0"), sem("att_in1")]
        recip_done, rd_high, rd_ready = sem("recip_done"), sem("rd_high"), sem("rd_ready")
        at_high, at_ready = sem("at_high"), sem("at_ready")
        xb_ready = sem("xb_ready")
        x2_high = sem("x2_high")
        tanh_done, ff_done, ff_high, fl_ready = sem("tanh_done"), sem("ff_done"), sem("ff_high"), sem("fl_ready")
        y_ready, stored = sem("y_ready"), [sem("stored0"), sem("stored1")]
        sp_passed, pool_passed, dve_passed, pe_passed = (sem(n) for n in ("sp_passed", "pool_passed", "dve_passed",
                                                                          "pe_passed"))

        mask_qk, mask_pad = mask_qk.bitcast(u8), mask_pad.bitcast(u8)
        x_v = x.rearrange("b (t p) f -> b p t f", p=P)
        c_v = ctx.rearrange("b (t p) f -> b p t f", p=P)
        o_v = out.rearrange("b (t p) f -> b t p f", p=P)
        slabs = ([(gate_w[k * P:(k + 1) * P, :], wg8[:, k, :]) for k in range(KT)]
                 + [(up_w[k * P:(k + 1) * P, :], wu8[:, k, :]) for k in range(KT)]
                 + [(down_w[3 * k * P:3 * (k + 1) * P, :].rearrange("(c p) n -> p c n", p=P),
                     wd8[:, 3 * k:3 * k + 3, :]) for k in range(KT)])

        def iterations(eng, steps):
            for r in (-2, -1, 0, 1):
                steps(r, r % 2)
            with eng.Fori(1, 3) as j:
                for odd in (0, 1):
                    steps(2 * j + odd, odd)
            for r in (6, 7, 8, 9):
                steps(r, r % 2)

        def pieces(r, par, step):
            for (name, n), at in WHEN.items():
                if at % STEPS == step and there(r, -(at // STEPS)):
                    yield name, n, r - at // STEPS, (par - at // STEPS) % 2

        def m_unit(r, step):
            u, k = step // 4, step % 4
            if k > 1:
                return None
            off, g = (0, 5 + u) if u < 3 else (1, u - 3)
            return (off, g, k) if there(r, off) else None

        block = es.enter_context(nc.Block())

        @block.sync
        def _(sp):
            def passed(s, n):
                past(sp, s, n)
                if not isinstance(n, int):
                    sp.sem_inc(sp_passed, 1)

            sp.dma_start(xin[:, :, :], x_v[0]).then_inc(ld_x, 16)
            sp.dma_start(ident[:, :], ident_in).then_inc(ld_ident, 16)
            sp.dma_start(st_q[:, :, :], Wq.rearrange("(t p) i -> p t i", p=P)).then_inc(ld_wq, 16)
            sp.dma_start(cin[:, :, :], c_v[0]).then_inc(ld_c, 16)
            sp.dma_start(st_k[:, :], Wk).then_inc(ld_wk, 16)
            sp.dma_start(st_v[:, :], Wv).then_inc(ld_wv, 16)
            sp.dma_start(mask_u8[:, :, :], mask_qk.rearrange("(t p) k -> p t k", p=P)).then_inc(ld_mask, 16)
            sp.dma_start(padc_u8[:, :], mask_pad.rearrange("b (t p) -> (b t) p", p=P)).then_inc(ld_mask, 16)
            sp.dma_start(rows_in[row_bq:row_bk, :], bq.rearrange("(t p) -> t p", p=P)).then_inc(ld_mask, 16)
            sp.dma_start(rows_in[row_bk:row_gs, :], bk.rearrange("(t p) -> t p", p=P)).then_inc(ld_mask, 16)
            sp.dma_start(rows_in[row_gs:row_us, :], gate_s.rearrange("(t p) -> t p", p=P)).then_inc(ld_mask, 16)
            sp.dma_start(rows_in[row_us:row_us + FT, :], up_s.rearrange("(t p) -> t p", p=P)).then_inc(ld_mask, 16)
            sp.dma_start(bv_b[:, :], bv.partition_broadcast(P)).then_inc(ld_small, 16)
            sp.dma_start(tg[:, 0:1], g_att.partition_broadcast(P)).then_inc(ld_small, 16)
            sp.dma_start(tg[:, 1:2], g_ffn.partition_broadcast(P)).then_inc(ld_small, 16)
            sp.dma_start(spread[:, :, :], spread_in).then_inc(ld_small, 16)
            sp.dma_start(tgbo[:, :], bo.partition_broadcast(P)).then_inc(ld_small, 16)
            sp.dma_start(dsb[:, :], down_s.partition_broadcast(P)).then_inc(ld_small, 16)
            sp.dma_start(padr_u8[:, :, :], mask_pad.partition_broadcast(P)).then_inc(ld_rows, 16)
            for s in range(2):
                sp.dma_start(st_f[s][:, :], slabs[s][0]).then_inc(ld_f[s], 16)
            sp.wait_ge(set_ready, 4)
            sp.dma_start(st_q[:, :, :], Wo.rearrange("(t p) i -> p t i", p=P)).then_inc(ld_wo, 16)

            for t in range(TT):
                sp.sem_inc(stored[t], 16)

            def slab(s):
                sp.wait_ge(f8_done, s - 1)
                dst = st_f[s % 2][:, :]
                if s >= 2 * KT:
                    dst = dst.rearrange("p (c n) -> p c n", c=3)
                sp.dma_start(dst, slabs[s][0]).then_inc(ld_f[s % 2], 16)

            def steps(r, par):
                for step in range(STEPS):
                    for name, n, b, odd in pieces(r, par, step):
                        first = isinstance(b, int) and b == 0
                        if name == "load_x" and not first:
                            passed(normed[0], 2 * b)
                            sp.dma_start(xin[:, :, :], x_v[b]).then_inc(ld_x, 16)
                        if name == "load_c" and not first:
                            passed(a_ready, A_USES * (b - 1) + 6)
                            sp.dma_start(cin[:, :, :], c_v[b]).then_inc(ld_c, 16)
                        if name == "load_xb":
                            passed(b_free, B_USES * (b - 1) + 4)
                            sp.dma_start(xb[:, :, :], x_v[b]).then_inc(ld_xb, 16)
                        if name == "put_q":
                            passed(a_free, A_USES * b + 4)
                            passed(qs_in, 96 * b)
                            for part, src in enumerate((qh, ql)):
                                sp.dma_start(q_dram[part].rearrange("(t p) n -> p t n", p=P),
                                             src[:, :, :]).then_inc(q_out, 16)
                        if name == "get_q":
                            passed(q_out, 32 * (b + 1))
                            passed(t_ready, 16 * (b - 1))
                            for hf in range(2):
                                for s in range(3):
                                    src = q_dram[(0, 1, 0)[s]].rearrange("(p f d) n -> f d p n", f=2, d=HD)[hf]
                                    sp.dma_start(qs[odd][64 * hf + HD * s:64 * hf + HD * (s + 1), :, :],
                                                 src).then_inc(qs_in, 16)
                        if name == "put_k":
                            passed(a_free, A_USES * b + 7)
                            passed(ks_in, 96 * b)
                            for part, src in enumerate((kh, kl)):
                                sp.dma_start(k_dram[part], src[:, :]).then_inc(k_out, 16)
                            passed(k_out, 32 * (b + 1))
                            passed(t_ready, 16 * (b - 1))
                            if isinstance(b, int) and b < 2:
                                sp.wait_ge(sm_rows, 1)
                            for hf in range(2):
                                for s in range(3):
                                    src = k_dram[(0, 0, 1)[s]].rearrange("(g d) n -> d g n", d=HD)
                                    sp.dma_start(ks[odd][64 * hf + HD * s:64 * hf + HD * (s + 1), :, :],
                                                 src).then_inc(ks_in, 16)
                        if name == "rows":
                            passed(mr_free, 2 * b + n + 1)
                            for v, rows in ((0, nm_h), (1, nm_l)):
                                for hf in range(2):
                                    row = 64 * hf + 3 * HD + v
                                    sp.dma_start(qs[odd][row:row + 1, 8 * n:8 * n + 8, :],
                                                 rows[8 * hf:8 * hf + 8, :]).then_inc(mr_in, 16)
                        if name == "den":
                            passed(un_ready, 8 * (b + 1))
                            passed(recip_done, b)
                            for j in range(HPG):
                                sp.dma_start(den[G * j:G * j + G, :],
                                             un[32 * j + HD:32 * j + HD + 1, :, :]).then_inc(den_in, 16)
                        if name == "gather":
                            passed(un_ready, 8 * b + 4 * n + 4)
                            passed(b_free, B_USES * (b - 1) + 2)
                            for gp in range(2):
                                for j in range(HPG):
                                    at = 64 * gp + HD * j
                                    sp.dma_start(att_u[at:at + HD, 2 * n:2 * n + 2, :],
                                                 un[32 * j:32 * j + HD, 4 * n + gp:4 * n + 4:2, :]
                                                 ).then_inc(att_in[n], 16)
                        if name == "store":
                            passed(y_ready, 2 * b + n + 1)
                            sp.dma_start(o_v[b][n], yt[:, n, :]).then_inc(stored[n], 16)
                    if isinstance(r, int) and (r == -1 or r == 0 and step < 16) and step % 4 == 3:
                        slab(2 + (step // 4 if r == -1 else 8 + step // 4)) if (r == 0 or step // 4 < 8) and \
                            2 + (step // 4 if r == -1 else 8 + step // 4) < len(slabs) else None
                if isinstance(r, int) and r == 9:
                    for t in range(TT):
                        sp.wait_ge(stored[t], 16 * (NB + 1))

            iterations(sp, steps)

        @block.gpsimd
        def _(pool):
            def passed(s, n):
                past(pool, s, n)
                if not isinstance(n, int):
                    pool.sem_inc(pool_passed, 1)

            pool.sem_inc(ff_done, RING)
            pool.sem_inc(fl_ready, RING)
            pool.memset(mhalf[:, :], -0.5)
            for i in range(2):
                last = pool.memset(va[i][:, :, :, HD:32], 1.0)
            last.then_inc(consts_pool, 1)
            pool.wait_ge(consts_pool, 1)

            def power(which, count):
                passed(vareps[which], count)
                pool.tensor_tensor(rs[which][:, :], ve[which][:, :], mhalf[:, :], ALU.pow).then_inc(rstd[which], 1)

            def pad_row(b, p_):
                if isinstance(b, int) and b == 0:
                    pool.wait_ge(ld_rows, 16)
                    pool.wait_ge(masks_f, 4)
                passed(mq_ready, 2 * b)
                pool.tensor_copy(padrow[:, :], padr_u8[:, b, :]).then_inc(mq_sum, 1)
                passed(mq_sum, 2 * b + 1)
                pool.tensor_scalar(padrow[:, :], padrow[:, :], -BIG, None, ALU.mult).then_inc(mq_sum, 1)
                passed(mq_sum, 2 * b + 2)
                passed(m_free, 16 * (b - 1))
                for t in range(TT):
                    pool.tensor_tensor(mq[p_][:, t, :], mask_q[:, t, :], padrow[:, :], ALU.add).then_inc(mq_ready, 1)

            def steps(r, par):
                for step in range(STEPS):
                    for name, n, b, odd in pieces(r, par, step):
                        if name == "pad_row":
                            pad_row(b, odd)
                        if name == "power":
                            power(n, b + 1)
                        if name == "fuse":
                            passed(c_free, C_USES * b + n + 1)
                            passed(fl_ready, FT * b + n + 1)
                            pool.tensor_tensor(ff[:, n % RING, :], ga[:, n % RING, :], up[:, n % RING, :],
                                               ALU.mult).then_inc(ff_done, 1)
                        if name == "fsplit":
                            split_low(b, n)
                        if name == "split_att":
                            passed(at_high, 2 * b + n + 1)
                            pool.tensor_tensor(at_l[:, 2 * n:2 * n + 2, :], att[:, 2 * n:2 * n + 2, :],
                                               at_h[:, 2 * n:2 * n + 2, :], ALU.subtract).then_inc(at_ready, 1)
                        if name == "add_y":
                            passed(c_free, C_USES * b + FT + n + 1)
                            pool.tensor_tensor(yt[:, n, :], yt[:, n, :], x2[odd][:, n, :], ALU.add).then_inc(y_ready, 1)
                        if name == "add_bo":
                            if isinstance(b, int) and b == 0:
                                pool.wait_ge(consts_dve, 1)
                            passed(ld_xb, 16 * (b + 1))
                            for t in range(TT):
                                last = pool.tensor_tensor(xb[:, t, :], xb[:, t, :], tgbo[:, :], ALU.add)
                            last.then_inc(xb_ready, 1)
                        if name == "padc":
                            if isinstance(b, int) and b == 0:
                                pool.wait_ge(consts_dve, 2)
                            passed(t_free, 16 * (b - 1))
                            cols = (padc_all[:, TT * b:TT * b + TT] if isinstance(b, int) else
                                    padc_all[:, bass.ds(TT * b, TT)])
                            pool.tensor_copy(padc[odd][:, :], cols).then_inc(padc_ready, 1)

            def split_low(b, c):
                passed(ff_high, FT * b + c + 1)
                if c == 0:
                    passed(c_ready, C_USES * b)
                pool.tensor_tensor(f_l[:, c, :], ff[:, c % RING, :], f_h[:, c, :], ALU.subtract).then_inc(fl_ready, 1)

            iterations(pool, steps)

        @block.scalar
        def _(act):
            def high(dst, src, scale, s, n):
                act.wait_ge(set_ready, n)
                act.activation(dst, src, ACT.Copy, scale=scale).then_inc(s, 1)

            act.wait_ge(ld_small, 96)
            act.activation(tg[:, :], tg[:, :], ACT.Tanh).then_inc(tanh_g, 1)

            def set_up(lo, hi):
                for n in range(lo, hi):
                    bank = sc[n % 4 // 2][:, D * (n % 2):D * (n % 2) + D]
                    if n < 4:
                        high(wq_h[:, n, :], bank, SWQK, set_high, n + 1)
                    elif n == 4:
                        high(wk_h[:, :, :], bank, SWQK, set_high, n + 1)
                    elif n == 5:
                        high(wv_h[:, :, :], bank, SWVO, set_high, n + 1)
                    elif n >= 8:
                        high(wo_h[:, n - 8, :], bank, SWVO, set_high, n + 1)

            def to_f8(s):
                act.wait_ge(ld_f[s % 2], 16 * (s // 2 + 1))
                src = st_f[s % 2][:, :]
                if s >= 2 * KT:
                    src = src.rearrange("p (c n) -> p c n", c=3)
                act.activation(slabs[s][1], src, ACT.Copy, saturate=False).then_inc(f8_done, 1)

            def steps(r, par):
                if isinstance(r, int) and r == -2:
                    set_up(0, SETUP_USES)
                for step in range(STEPS):
                    u = step // 4
                    if step == SUMS_AT and there(r, -1):
                        sums(r - 1, 7)
                    if step % 4 == SUMS_AT and u and there(r, 0):
                        sums(r, u - 1)
                    if step % 4 > 1 and there(r, 0):
                        n = 16 * r + 2 * u + step % 4 - 1
                        act.wait_ge(t_free, n)
                        unit = 2 * (u % 2) + step % 4 - 2
                        act.activation(ws[:, unit, :, :], ws[:, unit, :, :], ACT.Exp, scale=1.0 / SSC).then_inc(exp_done, 1)
                    for name, n, b, odd in pieces(r, par, step):
                        if name == "norm1":
                            past(act, shift[0], b + 1)
                            past(act, a_ready, 7 * (b - 1) + 2)
                            for t in range(TT):
                                act.activation(xn[:, t, :], xin[:, t, :], ACT.Identity, bias=nb_[0][:, t:t + 1],
                                               scale=rs[0][:, t:t + 1]).then_inc(normed[0], 1)
                        if name == "norm2":
                            past(act, shift[1], b + 1)
                            past(act, b_ready, B_USES * (b - 1) + 6)
                            for t in range(TT):
                                act.activation(x2n[:, t, :], x2[odd][:, t, :], ACT.Identity, bias=nb_[1][:, t:t + 1],
                                               scale=rs[1][:, t:t + 1]).then_inc(normed[1], 1)
                        if name == "xT":
                            act.wait_ge(a_ready, 7 * b + n + 1)
                            act.activation(xh[:, 2 * n:2 * n + 2, :], work[BANK[name, n]][:, :].rearrange("p (k l) -> p k l", k=2), ACT.Copy).then_inc(a_high, 1)
                        if name == "q":
                            if isinstance(b, int) and b == 0:
                                act.wait_ge(set_free, 8)
                            act.wait_ge(a_ready, 7 * b + n + 3)
                            past(act, q_out, 32 * b)
                            act.activation(qh[:, 2 * n, :], work[BANK[name, n]][:, 0:L], ACT.Identity, bias=bq_c[:, 2 * n:2 * n + 1])
                            act.activation(qh[:, 2 * n + 1, :], work[BANK[name, n]][:, L:2 * L], ACT.Identity,
                                           bias=bq_c[:, 2 * n + 1:2 * n + 2]).then_inc(a_high, 1)
                        if name == "cT":
                            act.wait_ge(a_ready, 7 * b + n + 5)
                            act.activation(ch[:, 2 * n:2 * n + 2, :], work[BANK[name, n]][:, :].rearrange("p (k l) -> p k l", k=2), ACT.Copy,
                                           scale=SX).then_inc(a_high, 1)
                        if name == "kv":
                            act.wait_ge(a_ready, 7 * b + 7)
                            past(act, k_out, 32 * b)
                            act.activation(kh[:, :], work[BANK[name, n]][:, 0:L], ACT.Identity, bias=bk_c[:, :]).then_inc(a_high, 1)
                        if name == "mrow":
                            act.wait_ge(mr_ready, 2 * b + n + 1)
                            past(act, mr_in, 64 * (2 * b + n))
                            act.activation(nm_h[:, :], av[0:H // 2, 0:L], ACT.Copy, scale=-1.0 / SM).then_inc(mr_high, 1)
                        if name == "split_att":
                            act.wait_ge(b_free, B_USES * b + n + 1)
                            past(act, b_ready, B_USES * (b - 1) + 4)
                            act.activation(at_h[:, 2 * n:2 * n + 2, :], att[:, 2 * n:2 * n + 2, :], ACT.Copy).then_inc(at_high, 1)
                        if name == "x2T":
                            act.wait_ge(b_ready, B_USES * b + n + 5)
                            past(act, c_ready, C_USES * (b - 1) + FT)
                            act.activation(h2_h[:, 2 * n:2 * n + 2, :], work[BANK[name, n]][:, :].rearrange("p (k l) -> p k l", k=2), ACT.Copy).then_inc(x2_high, 1)
                        if name == "gu":
                            act.wait_ge(c_ready, C_USES * b + n + 1)
                            act.wait_ge(ff_done, FT * b + n + 1)
                            act.activation(up[:, n % RING, :], work[BANK[name, n]][:, L:2 * L], ACT.Copy,
                                           scale=fuse_s[:, n:n + 1])
                            act.activation(th[:, n % RING, :], work[BANK[name, n]][:, 0:L], ACT.Tanh,
                                           scale=tanh_s[:, n:n + 1]).then_inc(tanh_done, 1)
                        if name == "fsplit":
                            split_high(b, n)
                    if isinstance(r, int) and (r == -1 or r == 0 and step < 16) and step % 4 == 3:
                        s = step // 4 + (0 if r == -1 else 8)
                        if s < len(slabs):
                            to_f8(s)

            def split_high(b, c):
                act.wait_ge(ff_done, RING + FT * b + c + 1)
                if c == 0:
                    past(act, c_ready, C_USES * b)
                act.activation(f_h[:, c, :], ff[:, c % RING, :], ACT.Copy).then_inc(ff_high, 1)

            def sums(b, g):
                act.wait_ge(av_ready, 8 * b + g + 1)
                past(act, att_in[g // 4], 128 * b)
                past(act, den_in, 64 * b)
                act.activation(un[:, g, :], av[:, 0:L], ACT.Copy).then_inc(un_ready, 1)

            iterations(act, steps)

        @block.vector
        def _(dve):
            def passed(s, n):
                past(dve, s, n)
                if not isinstance(n, int):
                    dve.sem_inc(dve_passed, 1)

            for i in range(2):
                for hf in range(2):
                    last = dve.memset(ks[i][64 * hf + 32:64 * hf + 64, :, :], SM)
            last.then_inc(sm_rows, 1)
            dve.wait_ge(ld_mask, 96)
            dve.tensor_copy(mask_f[:, :, :], mask_u8[:, :, :]).then_inc(masks_f, 1)
            dve.tensor_copy(rows_in[0:NB * TT, :], padc_u8[:, :]).then_inc(masks_f, 1)
            dve.wait_ge(masks_f, 1)
            dve.tensor_scalar(mask_q[:, :, :], mask_f[:, :, :], -BIG, None, ALU.mult).then_inc(masks_f, 2)
            dve.wait_ge(tanh_g, 1)
            dve.tensor_scalar(tgbo[:, :], tgbo[:, :], tg[:, 0:1], None, ALU.mult)
            dve.tensor_scalar(tgo[:, :], tg[:, 0:1], 1.0 / (SWVO * SA), None, ALU.mult)
            dve.tensor_scalar(dsb[:, :], dsb[:, :], tg[:, 1:2], 1.0 / SF, ALU.mult, ALU.mult).then_inc(consts_dve, 1)

            def set_up():
                for n in range(SETUP_USES):
                    bank = sc[n % 4 // 2][:, D * (n % 2):D * (n % 2) + D]
                    if n == 6:
                        dve.wait_ge(set_ready, n + 1)
                        dve.tensor_scalar(mask_k[:, :, :], bank.rearrange("p (t l) -> p t l", t=TT), -BIG, None, ALU.mult).then_inc(set_free, 1)
                        continue
                    if n == 7:
                        dve.wait_ge(set_ready, n + 1)
                        dve.tensor_scalar(padc_all[:, :], bank[:, 0:row_bq], -BIG, None, ALU.mult)
                        dve.tensor_scalar(bq_c[:, :], bank[:, row_bq:row_bk], SQK, None, ALU.mult)
                        dve.tensor_scalar(bk_c[:, :], bank[:, row_bk:row_gs], SQK, None, ALU.mult)
                        dve.tensor_scalar(tanh_s[:, :], bank[:, row_gs:row_us], 0.5 / SX, None, ALU.mult)
                        dve.tensor_scalar(gs_c[:, :], bank[:, row_gs:row_us], 0.5 * SF / (SX * SX), None,
                                          ALU.mult).then_inc(consts_dve, 1)
                        dve.wait_ge(consts_dve, 2)
                        dve.tensor_tensor(fuse_s[:, :], bank[:, row_us:row_us + FT], gs_c[:, :],
                                          ALU.mult).then_inc(set_free, 1)
                        continue
                    w_h, w_l, scale = ((wq_h[:, n, :], wq_l[:, n, :], SWQK) if n < 4 else
                                       (wk_h[:, :, :], wk_l[:, :, :], SWQK) if n == 4 else
                                       (wv_h[:, :, :], wv_l[:, :, :], SWVO) if n == 5 else
                                       (wo_h[:, n - 8, :], wo_l[:, n - 8, :], SWVO))
                    dve.wait_ge(set_high, n + 1 if n < 6 else n - 1)
                    dve.scalar_tensor_tensor(out=w_l, in0=bank, scalar=scale, in1=w_h, op0=ALU.mult,
                                             op1=ALU.subtract).then_inc(set_free, 1)

            def tile_stats(which, b, t, src):
                dve.bn_stats(bst[which][:, t, :], src[:, t, :]).then_inc(stats[which], 1)

            def piece(name, n, b, odd):
                if name == "stats1":
                    past(dve, ld_x, 16 * (b + 1))
                    for t in range(TT):
                        tile_stats(0, b, t, xin)
                    variance(0, b)
                if name in ("shift1", "shift2"):
                    i = int(name[-1]) - 1
                    dve.wait_ge(rstd[i], b + 1)
                    dve.scalar_tensor_tensor(out=nb_[i][:, :], in0=mv[i][:, :, 0], scalar=-1.0, in1=rs[i][:, :],
                                             op0=ALU.mult, op1=ALU.mult).then_inc(shift[i], 1)
                if name == "xT":
                    dve.wait_ge(a_high, 7 * b + n + 1)
                    dve.tensor_tensor(xl[:, 2 * n:2 * n + 2, :], work[BANK[name, n]][:, :].rearrange("p (k l) -> p k l", k=2),
                                      xh[:, 2 * n:2 * n + 2, :], ALU.subtract).then_inc(a_free, 1)
                if name == "q":
                    dve.wait_ge(a_high, 7 * b + n + 3)
                    dve.scalar_tensor_tensor(out=ql[:, 2 * n, :], in0=work[BANK[name, n]][:, 0:L], scalar=bq_c[:, 2 * n:2 * n + 1],
                                             in1=qh[:, 2 * n, :], op0=ALU.add, op1=ALU.subtract)
                    dve.scalar_tensor_tensor(out=ql[:, 2 * n + 1, :], in0=work[BANK[name, n]][:, L:2 * L], scalar=bq_c[:, 2 * n + 1:2 * n + 2],
                                             in1=qh[:, 2 * n + 1, :], op0=ALU.add, op1=ALU.subtract).then_inc(a_free, 1)
                if name == "cT":
                    dve.wait_ge(a_high, 7 * b + n + 5)
                    dve.scalar_tensor_tensor(out=cl[:, 2 * n:2 * n + 2, :], in0=work[BANK[name, n]][:, :].rearrange("p (k l) -> p k l", k=2),
                                             scalar=SX, in1=ch[:, 2 * n:2 * n + 2, :], op0=ALU.mult,
                                             op1=ALU.subtract).then_inc(a_free, 1)
                if name == "kv":
                    dve.wait_ge(a_high, 7 * b + 7)
                    dve.scalar_tensor_tensor(out=kl[:, :], in0=work[BANK[name, n]][:, 0:L], scalar=bk_c[:, :], in1=kh[:, :], op0=ALU.add,
                                             op1=ALU.subtract)
                    if isinstance(b, int) and b < 2:
                        dve.wait_ge(consts_pool, 1)
                    past(dve, av_ready, 8 * (b - 1))
                    for t in range(TT):
                        last = dve.scalar_tensor_tensor(
                            out=va[odd][:, t, :, 0:HD],
                            in0=work[BANK[name, n]][:, L + KV * t:L + KV * (t + 1)].rearrange("p (g d) -> p g d", d=HD),
                            scalar=1.0 / (SX * SWVO), in1=bv_b[:, :].rearrange("p (g d) -> p g d", d=HD),
                            op0=ALU.mult, op1=ALU.add)
                    last.then_inc(a_free, 1)
                if name == "mrow":
                    dve.wait_ge(mr_high, 2 * b + n + 1)
                    dve.scalar_tensor_tensor(out=nm_l[:, :], in0=av[0:H // 2, 0:L], scalar=-1.0 / SM, in1=nm_h[:, :],
                                             op0=ALU.mult, op1=ALU.subtract).then_inc(mr_free, 1)
                if name == "recip":
                    dve.wait_ge(den_in, 64 * (b + 1))
                    dve.reciprocal(rden[:, :], den[:, :]).then_inc(recip_done, 1)
                    dve.wait_ge(recip_done, b + 1)
                    past(dve, b_ready, B_USES * (b - 1) + 2)
                    dve.tensor_scalar(rd[0:H, :], rden[:, :], SA, None, ALU.mult).then_inc(rd_high, 1)
                    dve.wait_ge(rd_high, b + 1)
                    dve.scalar_tensor_tensor(out=rd[H:2 * H, :], in0=rden[:, :], scalar=SA, in1=rd[0:H, :], op0=ALU.mult,
                                             op1=ALU.subtract).then_inc(rd_ready, 1)
                if name == "spread":
                    dve.wait_ge(b_ready, B_USES * b + n + 1)
                    dve.wait_ge(att_in[n], 128 * (b + 1))
                    dve.tensor_tensor(att[:, 2 * n:2 * n + 2, :], work[BANK[name, n]][:, :].rearrange("p (k l) -> p k l", k=2),
                                      att_u[:, 2 * n:2 * n + 2, :], ALU.mult).then_inc(b_free, 1)
                if name == "out":
                    dve.wait_ge(b_ready, B_USES * b + n + 3)
                    dve.wait_ge(xb_ready, b + 1)
                    past(dve, y_ready, 2 * (b - 1))
                    dve.scalar_tensor_tensor(out=x2[odd][:, n, :], in0=work[BANK[name, n]][:, :], scalar=tgo[:, :], in1=xb[:, n, :],
                                             op0=ALU.mult, op1=ALU.add).then_inc(b_free, 1)
                    dve.wait_ge(b_free, B_USES * b + n + 3)
                    tile_stats(1, b, n, x2[odd])
                    if n == 1:
                        variance(1, b)
                if name == "x2T":
                    dve.wait_ge(x2_high, 2 * b + n + 1)
                    dve.tensor_tensor(h2_l[:, 2 * n:2 * n + 2, :], work[BANK[name, n]][:, :].rearrange("p (k l) -> p k l", k=2),
                                      h2_h[:, 2 * n:2 * n + 2, :], ALU.subtract).then_inc(b_free, 1)
                if name == "gu":
                    dve.wait_ge(tanh_done, FT * b + n + 1)
                    dve.wait_ge(ff_done, FT * b + n + 1)
                    dve.scalar_tensor_tensor(out=ga[:, n % RING, :], in0=th[:, n % RING, :], scalar=1.0,
                                             in1=work[BANK[name, n]][:, 0:L], op0=ALU.add,
                                             op1=ALU.mult).then_inc(c_free, 1)
                if name == "down_b":
                    dve.wait_ge(c_ready, C_USES * b + FT + n + 1)
                    dve.wait_ge(stored[n], 16 * (b + 1))
                    dve.tensor_tensor(yt[:, n, :], work[BANK["down", n]][:, :], dsb[:, :], ALU.mult).then_inc(c_free, 1)

            def variance(which, b):
                passed(stats[which], 2 * (b + 1))
                for t in range(TT):
                    last = dve.bn_aggr(mv[which][:, t, :], bst[which][:, t, :])
                last.then_inc(bnagg[which], 1)
                dve.wait_ge(bnagg[which], b + 1)
                dve.tensor_scalar(ve[which][:, :], mv[which][:, :, 1], 1e-5, 1.0 / (SX * SX), ALU.add,
                                  ALU.mult).then_inc(vareps[which], 1)

            def steps(r, par):
                if isinstance(r, int) and r == -2:
                    dve.wait_ge(ld_x, 16)
                    piece("stats1", 0, 0, 0)
                    dve.wait_ge(rstd[0], 1)
                    piece("shift1", 0, 0, 0)
                    set_up()
                for step in range(STEPS):
                    u, k = step // 4, step % 4
                    unit = m_unit(r, step)
                    if unit is not None:
                        off, g, t = unit
                        b, p_ = r + off, (par if off == 0 else 1 - par)
                        past(dve, mq_ready, 2 * (b + 1))
                        past(dve, m_free, 16 * b + 2 * g + t - 1)
                        passed(m_ready, 16 * b + 2 * g + t + 1)
                        for j in range(HPG):
                            pair, hf = 2 * g + j // 2, j % 2
                            col = 16 * (g // 4) + 8 * hf + pair % 8
                            last = dve.tensor_tensor_reduce(junk[:, HPG * t + j, :], sc[k][:, place(j)], mq[p_][:, t, :], 1.0,
                                                            -3.4e38, ALU.add, ALU.max, mx[:, t, col:col + 1])
                        last.then_inc(m_free, 1)
                    if k > 1 and there(r, 0):
                        kt = k - 2
                        past(dve, padc_ready, r + 1)
                        dve.wait_ge(t_ready, 16 * r + 2 * u + kt + 1)
                        past(dve, av_ready, 8 * r + u - 1)
                        dve.scalar_tensor_tensor(
                            out=ws[:, 2 * (u % 2) + kt, :, :], in0=sc[kt][:, :].rearrange("p (j l) -> p j l", j=HPG),
                            scalar=padc[par][:, kt:kt + 1], in1=mask_k[:, kt:kt + 1, :].broadcast_to([P, HPG, L]),
                            op0=ALU.add, op1=ALU.add).then_inc(t_free, 1)
                    late = pieces(r, par, step - 1) if step else pieces(r - 1, 1 - par, STEPS - 1)
                    for name, n, b, odd in late:
                        if isinstance(r, int) and r == -2 and name in ("stats1", "shift1"):
                            continue
                        piece(name, n, b, odd)

            iterations(dve, steps)

        @block.tensor
        def _(pe):
            mm = pe.matmul
            THREE = lambda wh, wl, dh, dl: ((wh, dh), (wh, dl), (wl, dh))

            def set_up():
                for n in range(SETUP_USES):
                    bank = sc[n % 4 // 2][:, D * (n % 2):D * (n % 2) + D]
                    if n >= 4:
                        pe.wait_ge(set_free, n - 3)
                    if n < 4 or n >= 8:
                        if n == 0:
                            pe.wait_ge(ld_ident, 16)
                            pe.wait_ge(ld_wq, 16)
                        if n == 8:
                            pe.wait_ge(ld_wo, 16)
                        k = n % 4
                        for t in range(KT):
                            last = pe.transpose(bank[:, t * P:(t + 1) * P], st_q[:, t, k * P:(k + 1) * P], ident[:, :])
                    elif n in (4, 5):
                        pe.wait_ge((ld_wk, ld_wv)[n - 4], 16)
                        st = (st_k, st_v)[n - 4]
                        for k in range(KT):
                            last = pe.transpose(bank[:, k * P:(k + 1) * P], st[:, k * P:(k + 1) * P], ident[:, :])
                    elif n == 6:
                        pe.wait_ge(masks_f, 2)
                        for kt in range(TT):
                            for t in range(TT):
                                last = pe.transpose(bank[:, kt * L + t * P:kt * L + (t + 1) * P],
                                                    mask_f[:, t, kt * P:(kt + 1) * P], ident[:, :])
                    else:
                        last = pe.transpose(bank[:, 0:row_us + FT], rows_in[:, :], ident[0:row_us + FT, 0:row_us + FT])
                    last.then_inc(set_ready, 1)

            def work_bank(piece, b):
                for chain, count in bank_waits(piece, b).items():
                    past(pe, {"a": a_free, "b": b_free, "c": c_free}[chain], count)
                return work[BANK[piece]]

            def maxima(b, g, t, p_, k):
                if g == 0 and t == 0:
                    pe.wait_ge(qs_in, 96 * (b + 1))
                    pe.wait_ge(ks_in, 96 * (b + 1))
                    if isinstance(b, int) and b == 0:
                        pe.wait_ge(set_free, SETUP_USES)
                past(pe, m_free, 16 * b + 2 * g - 1 + t)
                past(pe, t_free, 16 * (b - 1) + 2 * (g + 2) + t + 1 if g < 6 else 16 * b + 2 * (g - 6) + t + 1)
                for j in range(HPG):
                    pair, at = 2 * g + j // 2, 64 * (j % 2)
                    last = mm(sc[k][:, place(j)], qs[p_][at:at + 3 * HD, pair, t * P:(t + 1) * P],
                              ks[p_][at:at + 3 * HD, g, :], start=True, stop=True)
                last.then_inc(m_ready, 1)

            def scores(b, g, kt, p_):
                if g in (0, 4) and kt == 0:
                    pe.wait_ge(mr_in, 64 * (2 * b + g // 4 + 1))
                past(pe, t_free, 16 * b + 2 * g + kt - 1)
                done = 16 * b + 2 * (g + 5) + kt + 1
                past(pe, m_free, min(done, 16 * NB) if isinstance(done, int) else done)
                for j in range(HPG):
                    pair, at = 2 * g + j // 2, 64 * (j % 2)
                    last = mm(sc[kt][:, place(j)], ks[p_][at:at + 3 * HD + 2, g, kt * P:(kt + 1) * P],
                              qs[p_][at:at + 3 * HD + 2, pair, :], start=True, stop=True)
                last.then_inc(t_ready, 1)

            def weighted(b, g, p_):
                pe.wait_ge(exp_done, 16 * b + 2 * g + 2)
                past(pe, un_ready, 8 * b + g)
                rows = 2 * b + (1 if g < ROWS_AT[0] else 2 if g < ROWS_AT[1] else 3)
                past(pe, mr_free, min(rows, 2 * NB) if isinstance(rows, int) else rows)
                for kt in range(TT):
                    for j in range(HPG):
                        last = mm(av[32 * j:32 * (j + 1), 0:L], va[p_][:, kt, g, :],
                                  ws[:, 2 * (g % 2) + kt, 2 * (j % 2) + j // 2, :],
                                  start=kt == 0, stop=kt == TT - 1)
                last.then_inc(av_ready, 1)

            def piece(name, n, b):
                if name == "xT":
                    if n == 0:
                        pe.wait_ge(normed[0], 2 * (b + 1))
                    bank = work_bank((name, n), b)
                    for i in range(2):
                        for t in range(TT):
                            last = pe.transpose(bank[:, L * i + P * t:L * i + P * (t + 1)],
                                                xn[:, t, (2 * n + i) * P:(2 * n + i + 1) * P], ident[:, :])
                    last.then_inc(a_ready, 1)
                if name == "q":
                    bank = work_bank((name, n), b)
                    for i in range(2):
                        cols = slice((2 * n + i) * P, (2 * n + i + 1) * P)
                        for k in range(KT):
                            for s, (w, d) in enumerate(THREE(wq_h, wq_l, xh, xl)):
                                last = mm(bank[:, L * i:L * (i + 1)], w[:, k, cols], d[:, k, :], start=k == 0 and s == 0,
                                          stop=k == KT - 1 and s == 2)
                    last.then_inc(a_ready, 1)
                if name == "cT":
                    if n == 0:
                        pe.wait_ge(ld_c, 16 * (b + 1))
                    bank = work_bank((name, n), b)
                    for i in range(2):
                        for t in range(TT):
                            last = pe.transpose(bank[:, L * i + P * t:L * i + P * (t + 1)],
                                                cin[:, t, (2 * n + i) * P:(2 * n + i + 1) * P], ident[:, :])
                    last.then_inc(a_ready, 1)
                if name == "kv":
                    bank = work_bank((name, n), b)
                    for k in range(KT):
                        for s, (w, d) in enumerate(THREE(wk_h, wk_l, ch, cl)):
                            mm(bank[:, 0:L], w[:, k, :], d[:, k, :], start=k == 0 and s == 0, stop=k == KT - 1 and s == 2)
                    for t in range(TT):
                        for k in range(KT):
                            for s, (w, d) in enumerate(THREE(wv_h, wv_l, ch, cl)):
                                last = mm(bank[:, L + KV * t:L + KV * (t + 1)], d[:, k, t * P:(t + 1) * P], w[:, k, :],
                                          start=k == 0 and s == 0, stop=k == KT - 1 and s == 2)
                    last.then_inc(a_ready, 1)
                if name == "mrow":
                    pe.wait_ge(m_free, 16 * b + 8 * (n + 1))
                    past(pe, un_ready, 8 * b + ROWS_AT[0] if n == 1 else 8 * (b - 1) + ROWS_AT[1])
                    for t in range(TT):
                        last = pe.transpose(av[0:H // 2, P * t:P * (t + 1)], mx[:, t, 16 * n:16 * (n + 1)], ident[:, :])
                    last.then_inc(mr_ready, 1)
                if name == "spread":
                    if n == 0:
                        pe.wait_ge(rd_ready, b + 1)
                    bank = work_bank((name, n), b)
                    for i in range(2):
                        last = mm(bank[:, L * i:L * (i + 1)], spread[:, 2 * n + i, :], rd[:, :], start=True, stop=True)
                    last.then_inc(b_ready, 1)
                if name == "out":
                    if n == 0:
                        pe.wait_ge(at_ready, 2 * (b + 1))
                    bank = work_bank((name, n), b)
                    for k in range(KT):
                        for s, (d, w) in enumerate(((at_h, wo_h), (at_h, wo_l), (at_l, wo_h))):
                            last = mm(bank[:, :], d[:, k, n * P:(n + 1) * P], w[:, k, :], start=k == 0 and s == 0,
                                      stop=k == KT - 1 and s == 2)
                    last.then_inc(b_ready, 1)
                if name == "x2T":
                    if n == 0:
                        pe.wait_ge(normed[1], 2 * (b + 1))
                    bank = work_bank((name, n), b)
                    for i in range(2):
                        for t in range(TT):
                            last = pe.transpose(bank[:, L * i + P * t:L * i + P * (t + 1)],
                                                x2n[:, t, (2 * n + i) * P:(2 * n + i + 1) * P], ident[:, :])
                    last.then_inc(b_ready, 1)
                if name == "gu":
                    if n == 0 and isinstance(b, int) and b == 0:
                        pe.wait_ge(f8_done, len(slabs))
                    if n == 0:
                        pe.wait_ge(b_free, B_USES * b + 6)
                    bank = work_bank((name, n), b)
                    if not isinstance(b, int):
                        pe.sem_inc(pe_passed, 1)
                    for i, w in enumerate((wg8, wu8)):
                        for k in range(KT):
                            for s, d in enumerate((h2_h, h2_l)):
                                last = mm(bank[:, L * i:L * (i + 1)], w[:, k, n * P:(n + 1) * P], d[:, k, :],
                                          start=k == 0 and s == 0, stop=k == KT - 1 and s == 1)
                    last.then_inc(c_ready, 1)
                if name in ("down_a", "down_b"):
                    half = name == "down_b"
                    bank = work[BANK["down", n]] if half else work_bank(("down", n), b)
                    if n == 0:
                        pe.wait_ge(fl_ready, RING + FT * b + (FT if half else FT // 2))
                    if not isinstance(b, int):
                        pe.sem_inc(pe_passed, 1)
                    for c in range(FT // 2 * half, FT // 2 * (half + 1)):
                        for s, d in enumerate((f_h, f_l)):
                            last = mm(bank[:, :], d[:, c, n * P:(n + 1) * P], wd8[:, c, :], start=c == 0 and s == 0,
                                      stop=c == FT - 1 and s == 1)
                    if half:
                        last.then_inc(c_ready, 1)

            def steps(r, par):
                if isinstance(r, int) and r == -2:
                    set_up()
                for step in range(STEPS):
                    u, k = step // 4, step % 4
                    if step == SUMS_AT and there(r, -1):
                        weighted(r - 1, 7, 1 - par)
                    if k == SUMS_AT and u and there(r, 0):
                        weighted(r, u - 1, par)
                    unit = m_unit(r, step)
                    if unit is not None:
                        off, g, t = unit
                        maxima(r + off, g, t, par if off == 0 else 1 - par, k)
                    if k > 1 and there(r, 0):
                        scores(r, u, k - 2, par)
                    for name, n, b, odd in pieces(r, par, step):
                        piece(name, n, b)

            iterations(pe, steps)


_INS = ["x", "ctx_2048", "mask_SxS2_bc0", "mask_BxS2_bk0", "g_xattn", "g_ffn", "L0_xattn_Wq", "L0_xattn_bq",
        "L0_xattn_Wk", "L0_xattn_bk", "L0_xattn_Wv", "L0_xattn_bv", "L0_xattn_Wo", "L0_xattn_bo", "L0_ffn_gate_w",
        "L0_ffn_up_w", "L0_ffn_down_w", "L0_ffn_gate_scale", "L0_ffn_up_scale", "L0_ffn_down_scale"]


def kernel(**inputs):
    import numpy as np
    import concourse.bacc as bacc
    from concourse.bass_utils import run_bass_kernel_spmd

    nc = bacc.Bacc("TRN2", target_bir_lowering=False, num_devices=1)
    arrays, args = {}, []
    to = np.zeros((2, H, KT, P), np.float16)
    for g in range(G):
        for j in range(HPG):
            at = 64 * (g % 2) + HD * j
            to[:, j * G + g, g // 2, at:at + HD] = 1.0
    consts = {"ident": np.eye(P, dtype=np.float32), "spread": to.reshape(2 * H, KT, P)}
    for name in _INS + list(consts):
        a = np.ascontiguousarray(inputs[name] if name in inputs else consts[name])
        if a.dtype == np.bool_:
            a = a.view(np.uint32)
        arrays[f"in_{name}"] = a
        args.append(nc.dram_tensor(f"in_{name}", a.shape, mybir.dt.from_np(a.dtype), kind="ExternalInput").ap())
    args.append(nc.dram_tensor("out_x", (NB, L, D), mybir.dt.float32, kind="ExternalOutput").ap())
    xattn_ffn(nc, *args)
    r = run_bass_kernel_spmd(nc, [arrays], core_ids=[0])
    return r.results[0]["out_x"]
```

```python
import concourse.bass as bass
from concourse import mybir
from contextlib import ExitStack

NB, L, D = 8, 256, 512
H, G, HD = 32, 8, 16
HPG = H // G
F = 1536
P = 128
TT = L // P
KT = D // P
FT = F // P
PAIRS = H // 2
KV = G * HD

SX = 4.0
SWQK = 16.0
SWVO = 256.0
SQK = SX * SWQK
SSC = SQK * SQK * 4.0
SM = 2048.0
SA = 64.0
SF = 64.0
BIG = 1.0e30

STEPS = 32
SUMS_AT = (1, 2)
WHEN = {
    ("load_c", 0): -64, ("load_x", 0): -64, ("cT", 0): -60, ("cT", 1): -59, ("k", 0): -56, ("put_k", 0): -55,
    ("get_k", 0): -31, ("stats1", 0): -60, ("power", 0): -59, ("shift1", 0): -59, ("norm1", 0): -52,
    ("xT", 0): -50, ("xT", 1): -44, ("q", 0): -38, ("q", 1): -36, ("put_q", 0): -34, ("get_q", 0): -31,
    ("v", 0): -30, ("pad_row", 0): -30, ("padc", 0): -2, ("mrow", 0): -5, ("rows", 0): -4, ("mrow", 1): 11,
    ("rows", 1): 12, ("gather", 0): 19, ("den", 0): 35, ("gather", 1): 35, ("recip", 0): 38, ("load_xb", 0): 18,
    ("add_bo", 0): 21, ("spread", 0): 42, ("split_att", 0): 43, ("spread", 1): 44, ("split_att", 1): 46,
    ("out", 0): 48, ("out", 1): 50, ("power", 1): 51, ("shift2", 0): 51, ("norm2", 0): 53, ("x2T", 0): 54,
    ("x2T", 1): 56, **{("gu", c): 59 + 2 * c for c in range(FT)}, **{("fuse", c): 60 + 2 * c for c in range(FT)},
    **{("fsplit", c): 62 + 2 * c for c in range(FT)}, ("down_a", 0): 83, ("down_b", 0): 87, ("down_a", 1): 85,
    ("down_b", 1): 89, ("add_y", 0): 88, ("store", 0): 89, ("add_y", 1): 90, ("store", 1): 91,
}
ROWS_AT = ((WHEN["mrow", 1] - SUMS_AT[1]) // 4, (WHEN["mrow", 0] + STEPS - SUMS_AT[1]) // 4)
CHAINS = {
    "a": [("cT", 0), ("cT", 1), ("k", 0), ("xT", 0), ("xT", 1), ("q", 0), ("q", 1), ("v", 0)],
    "b": [("spread", 0), ("spread", 1), ("out", 0), ("out", 1), ("x2T", 0), ("x2T", 1)],
    "c": [("gu", c) for c in range(FT)] + [("down", 0), ("down", 1)],
}
A_USES, B_USES, C_USES = (len(chain) for chain in CHAINS.values())
A_HIGH = A_USES - 1
A_PLACE = {piece: n + 1 for n, piece in enumerate(CHAINS["a"])}
BANK = {
    **{piece: 0 for chain in "ab" for piece in CHAINS[chain]},
    **{piece: 1 + n % 2 for n, piece in enumerate(CHAINS["c"])},
    ("cT", 1): 1,
}
SETUP = ["Wk", "columns", "Wq0", "Wq1", "Wq2", "Wq3", "Wv", "mask", "Wo0", "Wo1", "Wo2", "Wo3"]
SETUP_AT = {0: (0, 2), 9: (2, 6), 22: (6, 8), 28: (8, 12)}
GATES_AT = 24
RING = 4


def bank_waits(piece, b):
    when = {**WHEN, ("down", 0): WHEN["down_a", 0], ("down", 1): WHEN["down_a", 1]}
    lines, counts = list(when), {}
    for name, chain in CHAINS.items():
        last = []
        for n, other in enumerate(chain):
            if BANK[other] == BANK[piece]:
                batches, apart = divmod(when[piece] - when[other], STEPS)
                if not apart and lines.index(other) >= lines.index(piece):
                    batches -= 1
                last.append(len(chain) * batches + n + 1)
        if last:
            count = len(chain) * b + max(last)
            counts[name] = min(count, len(chain) * NB) if isinstance(count, int) else count
    return counts


def three(w_h, w_l, d_h, d_l):
    return (w_h, d_h), (w_h, d_l), (w_l, d_h)


def past(eng, sem, count):
    if not isinstance(count, int) or count > 0:
        eng.wait_ge(sem, count)


def place(j):
    at = L * (2 * (j % 2) + j // 2)
    return slice(at, at + L)


def there(r, off):
    return not isinstance(r, int) or 0 <= r + off < NB


def xattn_ffn(nc, x, ctx, mask_qk, mask_pad, g_att, g_ffn, Wq, bq, Wk, bk, Wv, bv, Wo, bo,
              gate_w, up_w, down_w, gate_s, up_s, down_s, ident_in, spread_in, out):
    f32, f16, f8, u8 = mybir.dt.float32, mybir.dt.float16, mybir.dt.float8e4, mybir.dt.uint8
    ALU, ACT = mybir.AluOpType, mybir.ActivationFunctionType
    es = ExitStack()
    with es:
        def sb(name, shape, dt):
            return es.enter_context(nc.sbuf_tensor(name, shape, dt))

        def sem(name):
            return es.enter_context(nc.semaphore(name))

        wq_h, wq_l = sb("wq_h", [P, KT, D], f16), sb("wq_l", [P, KT, D], f16)
        wo_h, wo_l = sb("wo_h", [P, KT, D], f16), sb("wo_l", [P, KT, D], f16)
        wk_h, wk_l = sb("wk_h", [P, KT, KV], f16), sb("wk_l", [P, KT, KV], f16)
        wv_h, wv_l = sb("wv_h", [P, KT, KV], f16), sb("wv_l", [P, KT, KV], f16)
        wg8, wu8, wd8 = sb("wg8", [P, KT, F], f8), sb("wu8", [P, KT, F], f8), sb("wd8", [P, FT, D], f8)
        ident, spread = sb("ident", [P, P], f32), sb("spread", [2 * H, KT, P], f16)
        bq_c, bk_c, bv_b = sb("bq_c", [P, KT], f32), sb("bk_c", [P, 1], f32), sb("bv_b", [P, KV], f32)
        tg, tgo = sb("tg", [P, 2], f32), sb("tgo", [P, 1], f32)
        tgbo, dsb = sb("tgbo", [P, D], f32), sb("dsb", [P, D], f32)
        gs_c = sb("gs_c", [P, FT], f32)
        tanh_s, fuse_s = sb("tanh_s", [P, FT], f32), sb("fuse_s", [P, FT], f32)
        mhalf = sb("mhalf", [P, 2], f32)
        mask_u8 = sb("mask_u8", [P, TT, L], u8)
        mask_q, mask_k = sb("mask_q", [P, TT, L], f32), sb("mask_k", [P, TT, L], f32)
        padr_u8 = sb("padr_u8", [P, NB, L], u8)
        padc_u8, padc_all = sb("padc_u8", [NB * TT, P], u8), sb("padc_all", [P, NB * TT], f32)
        row_bq = NB * TT
        row_bk, row_gs = row_bq + KT, row_bq + KT + 1
        row_us = row_gs + FT
        rows_in = sb("rows_in", [row_us + FT, P], f32)
        xin, xn = sb("xin", [P, TT, D], f32), sb("xn", [P, TT, D], f32)
        cin = sb("cin", [P, TT, D], f32)
        xh, xl = sb("xh", [P, KT, L], f16), sb("xl", [P, KT, L], f16)
        ch, cl = sb("ch", [P, KT, L], f16), sb("cl", [P, KT, L], f16)
        qh, ql = sb("qh", [P, KT, L], f16), sb("ql", [P, KT, L], f16)
        kh, kl = sb("kh", [P, L], f16), sb("kl", [P, L], f16)
        qs = [sb(f"qs{i}", [P, PAIRS, L], f16) for i in range(2)]
        ks = [sb(f"ks{i}", [P, G, L], f16) for i in range(2)]
        va = [sb(f"va{i}", [P, TT, G, 32], f32) for i in range(2)]
        mq = [sb(f"mq{i}", [P, TT, L], f32) for i in range(2)]
        padrow = sb("padrow", [P, L], f32)
        padc = [sb(f"padc{i}", [P, TT], f32) for i in range(2)]
        mx, junk = sb("mx", [P, TT, H], f32), sb("junk", [P, 2 * HPG, L], mybir.dt.bfloat16)
        nm = sb("nm", [H // 2, L], f32)
        nm_h, nm_l = sb("nm_h", [H // 2, L], f16), sb("nm_l", [H // 2, L], f16)
        ws = sb("ws", [P, 4, HPG, L], f32)
        un = sb("un", [P, G, L], f32)
        att_u, att = sb("att_u", [P, KT, L], f32), sb("att", [P, KT, L], f32)
        den, rden = sb("den", [H, L], f32), sb("rden", [H, L], f32)
        rd = sb("rd", [2 * H, L], f16)
        at_h, at_l = sb("at_h", [P, KT, L], f16), sb("at_l", [P, KT, L], f16)
        xb, x2n = sb("xb", [P, TT, D], f32), sb("x2n", [P, TT, D], f32)
        x2 = [sb(f"x2_{i}", [P, TT, D], f32) for i in range(2)]
        h2_h, h2_l = sb("h2_h", [P, KT, L], f16), sb("h2_l", [P, KT, L], f16)
        th, ga = sb("th", [P, RING, L], f32), sb("ga", [P, RING, L], f32)
        up, ff = sb("up", [P, RING, L], f32), sb("ff", [P, RING, L], f32)
        f_h, f_l = sb("f_h", [P, FT, L], f16), sb("f_l", [P, FT, L], f16)
        yt = sb("yt", [P, TT, D], f32)
        bst = [sb(f"bst{i}", [P, TT, 6], f32) for i in range(2)]
        mv = [sb(f"mv{i}", [P, TT, 2], f32) for i in range(2)]
        ve = [sb(f"ve{i}", [P, TT], f32) for i in range(2)]
        rs = [sb(f"rs{i}", [P, TT], f32) for i in range(2)]
        nb_ = [sb(f"nb{i}", [P, TT], f32) for i in range(2)]

        st_q = un[:, :, :].rearrange("p (t a) l -> p t (a l)", t=KT)
        st_k = att_u[:, 0:2, :].rearrange("p a l -> p (a l)")
        st_v = att_u[:, 2:4, :].rearrange("p a l -> p (a l)")
        mask_f = att[:, 0:TT, :]
        st_f = [f[:, :, :].rearrange("p c l -> p (c l)").bitcast(f32) for f in (f_h, f_l)]

        sc = [es.enter_context(nc.psum_tensor(f"sc{i}", [P, 2 * D], f32)) for i in range(2)]
        av = es.enter_context(nc.psum_tensor("av", [P, D], f32))
        work = [es.enter_context(nc.psum_tensor(f"work{i}", [P, D], f32)) for i in range(3)]

        q_dram = nc.dram_tensor("q_scratch", [2, D, L], f16, kind="Internal").ap()
        k_dram = nc.dram_tensor("k_scratch", [2, KV, L], f16, kind="Internal").ap()

        ld_ident, ld_wq, ld_wk, ld_wv, ld_wo = sem("ld_ident"), sem("ld_wq"), sem("ld_wk"), sem("ld_wv"), sem("ld_wo")
        ld_mask, ld_cols, ld_small, ld_rows = sem("ld_mask"), sem("ld_cols"), sem("ld_small"), sem("ld_rows")
        ld_f = [sem("ld_f0"), sem("ld_f1")]
        f8_done = sem("f8_done")
        ld_x, ld_c, ld_xb = sem("ld_x"), sem("ld_c"), sem("ld_xb")
        set_ready, set_high, set_free = sem("set_ready"), sem("set_high"), sem("set_free")
        sm_rows, rows_f, masks_f = sem("sm_rows"), sem("rows_f"), sem("masks_f")
        gates_ready, columns_ready = sem("gates_ready"), sem("columns_ready")
        consts_pool, tanh_g = sem("consts_pool"), sem("tanh_g")
        a_ready, a_high, a_free = sem("a_ready"), sem("a_high"), sem("a_free")
        b_ready, b_free = sem("b_ready"), sem("b_free")
        c_ready, c_free = sem("c_ready"), sem("c_free")
        stats = [sem("stats1"), sem("stats2")]
        bnagg = [sem("bnagg1"), sem("bnagg2")]
        vareps = [sem("vareps1"), sem("vareps2")]
        rstd = [sem("rstd1"), sem("rstd2")]
        shift = [sem("shift1"), sem("shift2")]
        normed = [sem("normed1"), sem("normed2")]
        q_out, qs_in, k_out, ks_in = sem("q_out"), sem("qs_in"), sem("k_out"), sem("ks_in")
        mq_ready, mq_sum, padc_ready = sem("mq_ready"), sem("mq_sum"), sem("padc_ready")
        m_ready, m_free, t_ready, t_free = sem("m_ready"), sem("m_free"), sem("t_ready"), sem("t_free")
        exp_done, av_ready, un_ready = sem("exp_done"), sem("av_ready"), sem("un_ready")
        mr_ready, mr_high, mr_free, mr_in = sem("mr_ready"), sem("mr_high"), sem("mr_free"), sem("mr_in")
        den_in, att_in = sem("den_in"), [sem("att_in0"), sem("att_in1")]
        recip_done, rd_high, rd_ready = sem("recip_done"), sem("rd_high"), sem("rd_ready")
        at_high, at_ready = sem("at_high"), sem("at_ready")
        xb_ready = sem("xb_ready")
        x2_high = sem("x2_high")
        tanh_done, ff_done, ff_high, fl_ready = sem("tanh_done"), sem("ff_done"), sem("ff_high"), sem("fl_ready")
        y_ready, stored = sem("y_ready"), [sem("stored0"), sem("stored1")]
        sp_passed, pool_passed, dve_passed, pe_passed = (sem(n) for n in ("sp_passed", "pool_passed", "dve_passed",
                                                                          "pe_passed"))

        mask_qk, mask_pad = mask_qk.bitcast(u8), mask_pad.bitcast(u8)
        x_v = x.rearrange("b (t p) f -> b p t f", p=P)
        c_v = ctx.rearrange("b (t p) f -> b p t f", p=P)
        o_v = out.rearrange("b (t p) f -> b t p f", p=P)
        slabs = ([(gate_w[k * P:(k + 1) * P, :], wg8[:, k, :]) for k in range(KT)]
                 + [(up_w[k * P:(k + 1) * P, :], wu8[:, k, :]) for k in range(KT)]
                 + [(down_w[3 * k * P:3 * (k + 1) * P, :].rearrange("(c p) n -> p c n", p=P),
                     wd8[:, 3 * k:3 * k + 3, :]) for k in range(KT)])

        def iterations(eng, steps):
            for r in (-2, -1, 0, 1):
                steps(r, r % 2)
            with eng.Fori(1, 3) as j:
                for odd in (0, 1):
                    steps(2 * j + odd, odd)
            for r in (6, 7, 8, 9):
                steps(r, r % 2)

        def pieces(r, par, step):
            for (name, n), at in WHEN.items():
                if at % STEPS == step and there(r, -(at // STEPS)):
                    yield name, n, r - at // STEPS, (par - at // STEPS) % 2

        def bank_of(name, n):
            piece = ("down" if name == "down_b" else name, n)
            return work[BANK[piece]] if piece in BANK else None

        def halves(bank):
            return bank[:, :].rearrange("p (k l) -> p k l", k=2)

        def slab_at(r, step):
            n = 8 * (r + 1) + step // 4 if isinstance(r, int) and step % 4 == 3 else -1
            return n if 0 <= n < len(slabs) else None

        def m_unit(r, step):
            u, k = step // 4, step % 4
            if k > 1:
                return None
            off, g = (0, 5 + u) if u < 3 else (1, u - 3)
            return (off, g, k) if there(r, off) else None

        def weight(name):
            if name in ("Wk", "Wv"):
                return (wk_h[:, :, :], wk_l[:, :, :], SWQK) if name == "Wk" else (wv_h[:, :, :], wv_l[:, :, :], SWVO)
            k = int(name[2])
            return (wq_h[:, k, :], wq_l[:, k, :], SWQK) if name[1] == "q" else (wo_h[:, k, :], wo_l[:, k, :], SWVO)

        block = es.enter_context(nc.Block())

        @block.sync
        def _(sp):
            def passed(s, n):
                past(sp, s, n)
                if not isinstance(n, int):
                    sp.sem_inc(sp_passed, 1)

            sp.dma_start(ident[:, :], ident_in).then_inc(ld_ident, 16)
            sp.dma_start(st_k[:, :], Wk).then_inc(ld_wk, 16)
            sp.dma_start(cin[:, :, :], c_v[0]).then_inc(ld_c, 16)
            sp.dma_start(padc_u8[:, :], mask_pad.rearrange("b (t p) -> (b t) p", p=P)).then_inc(ld_cols, 16)
            sp.dma_start(rows_in[row_bq:row_bk, :], bq.rearrange("(t p) -> t p", p=P)).then_inc(ld_cols, 16)
            sp.dma_start(rows_in[row_bk:row_gs, :], bk.rearrange("(t p) -> t p", p=P)).then_inc(ld_cols, 16)
            sp.dma_start(rows_in[row_gs:row_us, :], gate_s.rearrange("(t p) -> t p", p=P)).then_inc(ld_cols, 16)
            sp.dma_start(rows_in[row_us:row_us + FT, :], up_s.rearrange("(t p) -> t p", p=P)).then_inc(ld_cols, 16)
            sp.dma_start(xin[:, :, :], x_v[0]).then_inc(ld_x, 16)
            sp.dma_start(st_q[:, :, :], Wq.rearrange("(t p) i -> p t i", p=P)).then_inc(ld_wq, 16)
            sp.dma_start(st_v[:, :], Wv).then_inc(ld_wv, 16)
            sp.dma_start(mask_u8[:, :, :], mask_qk.rearrange("(t p) k -> p t k", p=P)).then_inc(ld_mask, 16)
            sp.dma_start(bv_b[:, :], bv.partition_broadcast(P)).then_inc(ld_small, 16)
            sp.dma_start(tg[:, 0:1], g_att.partition_broadcast(P)).then_inc(ld_small, 16)
            sp.dma_start(tg[:, 1:2], g_ffn.partition_broadcast(P)).then_inc(ld_small, 16)
            sp.dma_start(spread[:, :, :], spread_in).then_inc(ld_small, 16)
            sp.dma_start(tgbo[:, :], bo.partition_broadcast(P)).then_inc(ld_small, 16)
            sp.dma_start(dsb[:, :], down_s.partition_broadcast(P)).then_inc(ld_small, 16)
            sp.dma_start(padr_u8[:, :, :], mask_pad.partition_broadcast(P)).then_inc(ld_rows, 16)
            for s in range(2):
                sp.dma_start(st_f[s][:, :], slabs[s][0]).then_inc(ld_f[s], 16)
            for t in range(TT):
                sp.sem_inc(stored[t], 16)

            def slab(s):
                sp.wait_ge(f8_done, s - 1)
                dst = st_f[s % 2][:, :]
                if s >= 2 * KT:
                    dst = dst.rearrange("p (c n) -> p c n", c=3)
                sp.dma_start(dst, slabs[s][0]).then_inc(ld_f[s % 2], 16)

            def steps(r, par):
                for step in range(STEPS):
                    if isinstance(r, int) and r == -2 and step == 8:
                        sp.wait_ge(a_ready, A_PLACE["cT", 1])
                        sp.dma_start(cin[:, :, :], c_v[1]).then_inc(ld_c, 16)
                    if isinstance(r, int) and r == -2 and step == 20:
                        sp.wait_ge(normed[0], 2)
                        sp.dma_start(xin[:, :, :], x_v[1]).then_inc(ld_x, 16)
                        sp.wait_ge(set_ready, 6)
                        sp.dma_start(st_q[:, :, :], Wo.rearrange("(t p) i -> p t i", p=P)).then_inc(ld_wo, 16)
                    for name, n, b, odd in pieces(r, par, step):
                        first = isinstance(b, int) and b < 2
                        if name == "load_x" and not first:
                            passed(normed[0], 2 * b)
                            sp.dma_start(xin[:, :, :], x_v[b]).then_inc(ld_x, 16)
                        if name == "load_c" and not first:
                            passed(a_ready, A_USES * (b - 1) + A_PLACE["cT", 1])
                            sp.dma_start(cin[:, :, :], c_v[b]).then_inc(ld_c, 16)
                        if name == "load_xb":
                            passed(b_free, B_USES * (b - 1) + 4)
                            sp.dma_start(xb[:, :, :], x_v[b]).then_inc(ld_xb, 16)
                        if name == "put_q":
                            passed(a_free, A_USES * b + A_PLACE["q", 1])
                            passed(qs_in, 96 * b)
                            for part, src in enumerate((qh, ql)):
                                sp.dma_start(q_dram[part].rearrange("(t p) n -> p t n", p=P),
                                             src[:, :, :]).then_inc(q_out, 16)
                        if name == "get_q":
                            passed(q_out, 32 * (b + 1))
                            passed(t_ready, 16 * (b - 1))
                            for hf in range(2):
                                for s in range(3):
                                    src = q_dram[(0, 1, 0)[s]].rearrange("(p f d) n -> f d p n", f=2, d=HD)[hf]
                                    sp.dma_start(qs[odd][64 * hf + HD * s:64 * hf + HD * (s + 1), :, :],
                                                 src).then_inc(qs_in, 16)
                        if name == "put_k":
                            passed(a_free, A_USES * b + A_PLACE["k", 0])
                            passed(ks_in, 96 * b)
                            for part, src in enumerate((kh, kl)):
                                sp.dma_start(k_dram[part], src[:, :]).then_inc(k_out, 16)
                        if name == "get_k":
                            passed(k_out, 32 * (b + 1))
                            passed(t_ready, 16 * (b - 1))
                            if isinstance(b, int) and b < 2:
                                sp.wait_ge(sm_rows, 2)
                            for hf in range(2):
                                for s in range(3):
                                    src = k_dram[(0, 0, 1)[s]].rearrange("(g d) n -> d g n", d=HD)
                                    sp.dma_start(ks[odd][64 * hf + HD * s:64 * hf + HD * (s + 1), :, :],
                                                 src).then_inc(ks_in, 16)
                        if name == "rows":
                            passed(mr_free, 2 * b + n + 1)
                            for v, rows in ((0, nm_h), (1, nm_l)):
                                for hf in range(2):
                                    row = 64 * hf + 3 * HD + v
                                    sp.dma_start(qs[odd][row:row + 1, 8 * n:8 * n + 8, :],
                                                 rows[8 * hf:8 * hf + 8, :]).then_inc(mr_in, 16)
                        if name == "den":
                            passed(un_ready, 8 * (b + 1))
                            passed(recip_done, b)
                            for j in range(HPG):
                                sp.dma_start(den[G * j:G * j + G, :],
                                             un[32 * j + HD:32 * j + HD + 1, :, :]).then_inc(den_in, 16)
                        if name == "gather":
                            passed(un_ready, 8 * b + 4 * n + 4)
                            passed(b_free, B_USES * (b - 1) + 2)
                            for gp in range(2):
                                for j in range(HPG):
                                    at = 64 * gp + HD * j
                                    sp.dma_start(att_u[at:at + HD, 2 * n:2 * n + 2, :],
                                                 un[32 * j:32 * j + HD, 4 * n + gp:4 * n + 4:2, :]
                                                 ).then_inc(att_in[n], 16)
                        if name == "store":
                            passed(y_ready, 2 * b + n + 1)
                            sp.dma_start(o_v[b][n], yt[:, n, :]).then_inc(stored[n], 16)
                    if slab_at(r, step) is not None and slab_at(r, step) + 2 < len(slabs):
                        slab(slab_at(r, step) + 2)
                if isinstance(r, int) and r == 9:
                    for t in range(TT):
                        sp.wait_ge(stored[t], 16 * (NB + 1))

            iterations(sp, steps)

        @block.gpsimd
        def _(pool):
            def passed(s, n):
                past(pool, s, n)
                if not isinstance(n, int):
                    pool.sem_inc(pool_passed, 1)

            pool.sem_inc(ff_done, RING)
            pool.sem_inc(fl_ready, RING)
            pool.memset(mhalf[:, :], -0.5)
            for i in range(2):
                last = pool.memset(va[i][:, :, :, HD:32], 1.0)
            last.then_inc(consts_pool, 1)
            for i in range(2):
                pool.memset(ks[i][:, :, :], SM).then_inc(sm_rows, 1)
            pool.wait_ge(consts_pool, 1)

            def power(which, count):
                passed(vareps[which], count)
                pool.tensor_tensor(rs[which][:, :], ve[which][:, :], mhalf[:, :], ALU.pow).then_inc(rstd[which], 1)

            def pad_row(b, p_):
                if isinstance(b, int) and b == 0:
                    pool.wait_ge(ld_rows, 16)
                    pool.wait_ge(masks_f, 2)
                passed(mq_ready, 2 * b)
                pool.tensor_copy(padrow[:, :], padr_u8[:, b, :]).then_inc(mq_sum, 1)
                passed(mq_sum, 2 * b + 1)
                pool.tensor_scalar(padrow[:, :], padrow[:, :], -BIG, None, ALU.mult).then_inc(mq_sum, 1)
                passed(mq_sum, 2 * b + 2)
                passed(m_free, 16 * (b - 1))
                for t in range(TT):
                    pool.tensor_tensor(mq[p_][:, t, :], mask_q[:, t, :], padrow[:, :], ALU.add).then_inc(mq_ready, 1)

            def steps(r, par):
                for step in range(STEPS):
                    for name, n, b, odd in pieces(r, par, step):
                        if name == "pad_row":
                            pad_row(b, odd)
                        if name == "power":
                            power(n, b + 1)
                        if name == "fuse":
                            passed(c_free, C_USES * b + n + 1)
                            passed(fl_ready, FT * b + n + 1)
                            pool.tensor_tensor(ff[:, n % RING, :], ga[:, n % RING, :], up[:, n % RING, :],
                                               ALU.mult).then_inc(ff_done, 1)
                        if name == "fsplit":
                            split_low(b, n)
                        if name == "mrow":
                            passed(mr_high, 2 * b + n + 1)
                            pool.tensor_tensor(nm_l[:, :], nm[:, :], nm_h[:, :], ALU.subtract).then_inc(mr_free, 1)
                        if name == "split_att":
                            passed(at_high, 2 * b + n + 1)
                            pool.tensor_tensor(at_l[:, 2 * n:2 * n + 2, :], att[:, 2 * n:2 * n + 2, :],
                                               at_h[:, 2 * n:2 * n + 2, :], ALU.subtract).then_inc(at_ready, 1)
                        if name == "add_y":
                            passed(c_free, C_USES * b + FT + n + 1)
                            pool.tensor_tensor(yt[:, n, :], yt[:, n, :], x2[odd][:, n, :],
                                               ALU.add).then_inc(y_ready, 1)
                        if name == "add_bo":
                            if isinstance(b, int) and b == 0:
                                pool.wait_ge(gates_ready, 1)
                            passed(ld_xb, 16 * (b + 1))
                            for t in range(TT):
                                last = pool.tensor_tensor(xb[:, t, :], xb[:, t, :], tgbo[:, :], ALU.add)
                            last.then_inc(xb_ready, 1)
                        if name == "padc":
                            if isinstance(b, int) and b == 0:
                                pool.wait_ge(columns_ready, 1)
                            passed(t_free, 16 * (b - 1))
                            cols = (padc_all[:, TT * b:TT * b + TT] if isinstance(b, int) else
                                    padc_all[:, bass.ds(TT * b, TT)])
                            pool.tensor_copy(padc[odd][:, :], cols).then_inc(padc_ready, 1)

            def split_low(b, c):
                passed(ff_high, FT * b + c + 1)
                if c == 0:
                    passed(c_ready, C_USES * b)
                pool.tensor_tensor(f_l[:, c, :], ff[:, c % RING, :], f_h[:, c, :], ALU.subtract).then_inc(fl_ready, 1)

            iterations(pool, steps)

        @block.scalar
        def _(act):
            def set_up(first, behind):
                for n in range(first, behind):
                    bank = sc[n % 4 // 2][:, D * (n % 2):D * (n % 2) + D]
                    if SETUP[n][0] == "W":
                        w_h, _, scale = weight(SETUP[n])
                        act.wait_ge(set_ready, n + 1)
                        act.activation(w_h, bank, ACT.Copy, scale=scale).then_inc(set_high, 1)

            def to_f8(s):
                act.wait_ge(ld_f[s % 2], 16 * (s // 2 + 1))
                src = st_f[s % 2][:, :]
                if s >= 2 * KT:
                    src = src.rearrange("p (c n) -> p c n", c=3)
                act.activation(slabs[s][1], src, ACT.Copy, saturate=False).then_inc(f8_done, 1)

            def steps(r, par):
                for step in range(STEPS):
                    u = step // 4
                    if isinstance(r, int) and r == -2 and step in SETUP_AT:
                        set_up(*SETUP_AT[step])
                    if isinstance(r, int) and r == -2 and step == GATES_AT:
                        act.wait_ge(ld_small, 96)
                        act.activation(tg[:, :], tg[:, :], ACT.Tanh).then_inc(tanh_g, 1)
                    if step == SUMS_AT[1] and there(r, -1):
                        sums(r - 1, 7)
                    if step % 4 == SUMS_AT[1] and u and there(r, 0):
                        sums(r, u - 1)
                    for name, n, b, odd in pieces(r, par, step):
                        bank = bank_of(name, n)
                        if name == "norm1":
                            past(act, shift[0], b + 1)
                            past(act, a_ready, A_USES * (b - 1) + A_PLACE["xT", 1])
                            for t in range(TT):
                                act.activation(xn[:, t, :], xin[:, t, :], ACT.Identity, bias=nb_[0][:, t:t + 1],
                                               scale=rs[0][:, t:t + 1]).then_inc(normed[0], 1)
                        if name == "norm2":
                            past(act, shift[1], b + 1)
                            past(act, b_ready, B_USES * (b - 1) + 6)
                            for t in range(TT):
                                act.activation(x2n[:, t, :], x2[odd][:, t, :], ACT.Identity, bias=nb_[1][:, t:t + 1],
                                               scale=rs[1][:, t:t + 1]).then_inc(normed[1], 1)
                        if name == "xT":
                            act.wait_ge(a_ready, A_USES * b + A_PLACE[name, n])
                            act.activation(xh[:, 2 * n:2 * n + 2, :], halves(bank), ACT.Copy).then_inc(a_high, 1)
                        if name == "q":
                            act.wait_ge(a_ready, A_USES * b + A_PLACE[name, n])
                            past(act, q_out, 32 * b)
                            act.activation(qh[:, 2 * n, :], bank[:, 0:L], ACT.Identity, bias=bq_c[:, 2 * n:2 * n + 1])
                            act.activation(qh[:, 2 * n + 1, :], bank[:, L:2 * L], ACT.Identity,
                                           bias=bq_c[:, 2 * n + 1:2 * n + 2]).then_inc(a_high, 1)
                        if name == "cT":
                            act.wait_ge(a_ready, A_USES * b + A_PLACE[name, n])
                            act.activation(ch[:, 2 * n:2 * n + 2, :], halves(bank), ACT.Copy,
                                           scale=SX).then_inc(a_high, 1)
                        if name == "k":
                            if isinstance(b, int) and b == 0:
                                act.wait_ge(set_free, 2)
                            act.wait_ge(a_ready, A_USES * b + A_PLACE[name, n])
                            past(act, k_out, 32 * b)
                            act.activation(kh[:, :], bank[:, 0:L], ACT.Identity, bias=bk_c[:, :]).then_inc(a_high, 1)
                        if name == "mrow":
                            act.wait_ge(mr_ready, 2 * b + n + 1)
                            past(act, mr_in, 64 * (2 * b + n))
                            act.activation(nm[:, :], av[0:H // 2, 0:L], ACT.Copy, scale=-1.0 / SM)
                            act.activation(nm_h[:, :], av[0:H // 2, 0:L], ACT.Copy,
                                           scale=-1.0 / SM).then_inc(mr_high, 1)
                        if name == "split_att":
                            act.wait_ge(b_free, B_USES * b + n + 1)
                            past(act, b_ready, B_USES * (b - 1) + 4)
                            act.activation(at_h[:, 2 * n:2 * n + 2, :], att[:, 2 * n:2 * n + 2, :],
                                           ACT.Copy).then_inc(at_high, 1)
                        if name == "x2T":
                            act.wait_ge(b_ready, B_USES * b + n + 5)
                            past(act, c_ready, C_USES * (b - 1) + FT)
                            act.activation(h2_h[:, 2 * n:2 * n + 2, :], halves(bank), ACT.Copy).then_inc(x2_high, 1)
                        if name == "gu":
                            act.wait_ge(c_ready, C_USES * b + n + 1)
                            act.wait_ge(ff_done, FT * b + n + 1)
                            act.activation(up[:, n % RING, :], bank[:, L:2 * L], ACT.Copy,
                                           scale=fuse_s[:, n:n + 1])
                            act.activation(th[:, n % RING, :], bank[:, 0:L], ACT.Tanh,
                                           scale=tanh_s[:, n:n + 1]).then_inc(tanh_done, 1)
                        if name == "fsplit":
                            split_high(b, n)
                    if step % 4 > 1 and there(r, 0):
                        n = 16 * r + 2 * u + step % 4 - 1
                        act.wait_ge(t_free, n)
                        unit = 2 * (u % 2) + step % 4 - 2
                        act.activation(ws[:, unit, :, :], ws[:, unit, :, :], ACT.Exp,
                                       scale=1.0 / SSC).then_inc(exp_done, 1)
                    if slab_at(r, step) is not None:
                        to_f8(slab_at(r, step))

            def split_high(b, c):
                act.wait_ge(ff_done, RING + FT * b + c + 1)
                if c == 0:
                    past(act, c_ready, C_USES * b)
                act.activation(f_h[:, c, :], ff[:, c % RING, :], ACT.Copy).then_inc(ff_high, 1)

            def sums(b, g):
                act.wait_ge(av_ready, 8 * b + g + 1)
                past(act, att_in[g // 4], 128 * b)
                past(act, den_in, 64 * b)
                act.activation(un[:, g, :], av[:, 0:L], ACT.Copy).then_inc(un_ready, 1)

            iterations(act, steps)

        @block.vector
        def _(dve):
            def passed(s, n):
                past(dve, s, n)
                if not isinstance(n, int):
                    dve.sem_inc(dve_passed, 1)

            def gates():
                dve.wait_ge(tanh_g, 1)
                dve.tensor_scalar(tgbo[:, :], tgbo[:, :], tg[:, 0:1], None, ALU.mult)
                dve.tensor_scalar(tgo[:, :], tg[:, 0:1], 1.0 / (SWVO * SA), None, ALU.mult)
                dve.tensor_scalar(dsb[:, :], dsb[:, :], tg[:, 1:2], 1.0 / SF, ALU.mult,
                                  ALU.mult).then_inc(gates_ready, 1)

            def set_up(first, behind):
                for n in range(first, behind):
                    bank = sc[n % 4 // 2][:, D * (n % 2):D * (n % 2) + D]
                    if SETUP[n] == "mask":
                        dve.wait_ge(set_ready, n + 1)
                        dve.tensor_scalar(mask_k[:, :, :], bank.rearrange("p (t l) -> p t l", t=TT), -BIG, None,
                                          ALU.mult).then_inc(set_free, 1)
                        dve.tensor_scalar(mask_q[:, :, :], mask_f[:, :, :], -BIG, None, ALU.mult).then_inc(masks_f, 1)
                    elif SETUP[n] == "columns":
                        dve.wait_ge(set_ready, n + 1)
                        dve.tensor_scalar(padc_all[:, :], bank[:, 0:row_bq], -BIG, None, ALU.mult)
                        dve.tensor_scalar(bq_c[:, :], bank[:, row_bq:row_bk], SQK, None, ALU.mult)
                        dve.tensor_scalar(bk_c[:, :], bank[:, row_bk:row_gs], SQK, None, ALU.mult)
                        dve.tensor_scalar(tanh_s[:, :], bank[:, row_gs:row_us], 0.5 / SX, None, ALU.mult)
                        dve.tensor_scalar(gs_c[:, :], bank[:, row_gs:row_us], 0.5 * SF / (SX * SX), None,
                                          ALU.mult).then_inc(columns_ready, 1)
                        dve.wait_ge(columns_ready, 1)
                        dve.tensor_tensor(fuse_s[:, :], bank[:, row_us:row_us + FT], gs_c[:, :],
                                          ALU.mult).then_inc(set_free, 1)
                    else:
                        w_h, w_l, scale = weight(SETUP[n])
                        dve.wait_ge(set_high, sum(name[0] == "W" for name in SETUP[:n + 1]))
                        dve.scalar_tensor_tensor(out=w_l, in0=bank, scalar=scale, in1=w_h, op0=ALU.mult,
                                                 op1=ALU.subtract).then_inc(set_free, 1)

            dve.wait_ge(ld_cols, 80)
            dve.tensor_copy(rows_in[0:NB * TT, :], padc_u8[:, :]).then_inc(rows_f, 1)

            def tile_stats(which, b, t, src):
                dve.bn_stats(bst[which][:, t, :], src[:, t, :]).then_inc(stats[which], 1)

            def piece(name, n, b, odd):
                bank = bank_of(name, n)
                if name == "stats1":
                    past(dve, ld_x, 16 * (b + 1))
                    for t in range(TT):
                        tile_stats(0, b, t, xin)
                    variance(0, b)
                if name in ("shift1", "shift2"):
                    i = int(name[-1]) - 1
                    dve.wait_ge(rstd[i], b + 1)
                    dve.scalar_tensor_tensor(out=nb_[i][:, :], in0=mv[i][:, :, 0], scalar=-1.0, in1=rs[i][:, :],
                                             op0=ALU.mult, op1=ALU.mult).then_inc(shift[i], 1)
                if name == "xT":
                    dve.wait_ge(a_high, A_HIGH * b + A_PLACE[name, n])
                    dve.tensor_tensor(xl[:, 2 * n:2 * n + 2, :], halves(bank),
                                      xh[:, 2 * n:2 * n + 2, :], ALU.subtract).then_inc(a_free, 1)
                if name == "q":
                    dve.wait_ge(a_high, A_HIGH * b + A_PLACE[name, n])
                    for i in range(2):
                        k = 2 * n + i
                        last = dve.scalar_tensor_tensor(out=ql[:, k, :], in0=bank[:, L * i:L * (i + 1)],
                                                        scalar=bq_c[:, k:k + 1], in1=qh[:, k, :], op0=ALU.add,
                                                        op1=ALU.subtract)
                    last.then_inc(a_free, 1)
                if name == "cT":
                    dve.wait_ge(a_high, A_HIGH * b + A_PLACE[name, n])
                    dve.scalar_tensor_tensor(out=cl[:, 2 * n:2 * n + 2, :], in0=halves(bank),
                                             scalar=SX, in1=ch[:, 2 * n:2 * n + 2, :], op0=ALU.mult,
                                             op1=ALU.subtract).then_inc(a_free, 1)
                if name == "k":
                    dve.wait_ge(a_high, A_HIGH * b + A_PLACE[name, n])
                    dve.scalar_tensor_tensor(out=kl[:, :], in0=bank[:, 0:L], scalar=bk_c[:, :],
                                             in1=kh[:, :], op0=ALU.add, op1=ALU.subtract).then_inc(a_free, 1)
                if name == "v":
                    dve.wait_ge(a_ready, A_USES * b + A_PLACE[name, n])
                    if isinstance(b, int) and b < 2:
                        dve.wait_ge(consts_pool, 1)
                    past(dve, av_ready, 8 * (b - 1))
                    for t in range(TT):
                        last = dve.scalar_tensor_tensor(
                            out=va[odd][:, t, :, 0:HD],
                            in0=bank[:, KV * t:KV * (t + 1)].rearrange("p (g d) -> p g d", d=HD),
                            scalar=1.0 / (SX * SWVO), in1=bv_b[:, :].rearrange("p (g d) -> p g d", d=HD),
                            op0=ALU.mult, op1=ALU.add)
                    last.then_inc(a_free, 1)
                if name == "recip":
                    dve.wait_ge(den_in, 64 * (b + 1))
                    dve.reciprocal(rden[:, :], den[:, :]).then_inc(recip_done, 1)
                    dve.wait_ge(recip_done, b + 1)
                    past(dve, b_ready, B_USES * (b - 1) + 2)
                    dve.tensor_scalar(rd[0:H, :], rden[:, :], SA, None, ALU.mult).then_inc(rd_high, 1)
                    dve.wait_ge(rd_high, b + 1)
                    dve.scalar_tensor_tensor(out=rd[H:2 * H, :], in0=rden[:, :], scalar=SA, in1=rd[0:H, :],
                                             op0=ALU.mult, op1=ALU.subtract).then_inc(rd_ready, 1)
                if name == "spread":
                    dve.wait_ge(b_ready, B_USES * b + n + 1)
                    dve.wait_ge(att_in[n], 128 * (b + 1))
                    dve.tensor_tensor(att[:, 2 * n:2 * n + 2, :], halves(bank),
                                      att_u[:, 2 * n:2 * n + 2, :], ALU.mult).then_inc(b_free, 1)
                if name == "out":
                    dve.wait_ge(b_ready, B_USES * b + n + 3)
                    dve.wait_ge(xb_ready, b + 1)
                    past(dve, y_ready, 2 * (b - 1))
                    dve.scalar_tensor_tensor(out=x2[odd][:, n, :], in0=bank[:, :], scalar=tgo[:, :], in1=xb[:, n, :],
                                             op0=ALU.mult, op1=ALU.add).then_inc(b_free, 1)
                    dve.wait_ge(b_free, B_USES * b + n + 3)
                    tile_stats(1, b, n, x2[odd])
                    if n == 1:
                        variance(1, b)
                if name == "x2T":
                    dve.wait_ge(x2_high, 2 * b + n + 1)
                    dve.tensor_tensor(h2_l[:, 2 * n:2 * n + 2, :], halves(bank),
                                      h2_h[:, 2 * n:2 * n + 2, :], ALU.subtract).then_inc(b_free, 1)
                if name == "gu":
                    dve.wait_ge(tanh_done, FT * b + n + 1)
                    dve.wait_ge(ff_done, FT * b + n + 1)
                    dve.scalar_tensor_tensor(out=ga[:, n % RING, :], in0=th[:, n % RING, :], scalar=1.0,
                                             in1=bank[:, 0:L], op0=ALU.add,
                                             op1=ALU.mult).then_inc(c_free, 1)
                if name == "down_b":
                    dve.wait_ge(c_ready, C_USES * b + FT + n + 1)
                    dve.wait_ge(stored[n], 16 * (b + 1))
                    dve.tensor_tensor(yt[:, n, :], bank[:, :], dsb[:, :], ALU.mult).then_inc(c_free, 1)

            def variance(which, b):
                passed(stats[which], 2 * (b + 1))
                for t in range(TT):
                    last = dve.bn_aggr(mv[which][:, t, :], bst[which][:, t, :])
                last.then_inc(bnagg[which], 1)
                dve.wait_ge(bnagg[which], b + 1)
                dve.tensor_scalar(ve[which][:, :], mv[which][:, :, 1], 1e-5, 1.0 / (SX * SX), ALU.add,
                                  ALU.mult).then_inc(vareps[which], 1)

            def steps(r, par):
                for step in range(STEPS):
                    u, k = step // 4, step % 4
                    unit = m_unit(r, step)
                    if unit is not None:
                        off, g, t = unit
                        b, p_ = r + off, (par if off == 0 else 1 - par)
                        past(dve, mq_ready, 2 * (b + 1))
                        past(dve, m_free, 16 * b + 2 * g + t - 1)
                        passed(m_ready, 16 * b + 2 * g + t + 1)
                        for j in range(HPG):
                            pair, hf = 2 * g + j // 2, j % 2
                            col = 16 * (g // 4) + 8 * hf + pair % 8
                            last = dve.tensor_tensor_reduce(junk[:, HPG * t + j, :], sc[k][:, place(j)],
                                                            mq[p_][:, t, :], 1.0, -3.4e38, ALU.add, ALU.max,
                                                            mx[:, t, col:col + 1])
                        last.then_inc(m_free, 1)
                    if k > 1 and there(r, 0):
                        kt = k - 2
                        past(dve, padc_ready, r + 1)
                        dve.wait_ge(t_ready, 16 * r + 2 * u + kt + 1)
                        past(dve, av_ready, 8 * r + u - 1)
                        dve.scalar_tensor_tensor(
                            out=ws[:, 2 * (u % 2) + kt, :, :], in0=sc[kt][:, :].rearrange("p (j l) -> p j l", j=HPG),
                            scalar=padc[par][:, kt:kt + 1], in1=mask_k[:, kt:kt + 1, :].broadcast_to([P, HPG, L]),
                            op0=ALU.add, op1=ALU.add).then_inc(t_free, 1)
                    late = pieces(r, par, step - 1) if step else pieces(r - 1, 1 - par, STEPS - 1)
                    for name, n, b, odd in late:
                        piece(name, n, b, odd)
                    if isinstance(r, int) and r == -2:
                        if step == 14:
                            dve.wait_ge(ld_mask, 16)
                            dve.tensor_copy(mask_f[:, :, :], mask_u8[:, :, :]).then_inc(masks_f, 1)
                            dve.wait_ge(masks_f, 1)
                        if step in SETUP_AT:
                            set_up(*SETUP_AT[step])
                        if step == GATES_AT:
                            gates()

            iterations(dve, steps)

        @block.tensor
        def _(pe):
            mm = pe.matmul

            def set_up(first, behind):
                for n in range(first, behind):
                    bank = sc[n % 4 // 2][:, D * (n % 2):D * (n % 2) + D]
                    if n >= 4:
                        pe.wait_ge(set_free, n - 3)
                    if n == 0:
                        pe.wait_ge(ld_ident, 16)
                    if SETUP[n] in ("Wq0", "Wo0"):
                        pe.wait_ge(ld_wq if SETUP[n] == "Wq0" else ld_wo, 16)
                    if SETUP[n] in ("Wk", "Wv"):
                        pe.wait_ge(ld_wk if SETUP[n] == "Wk" else ld_wv, 16)
                        st = st_k if SETUP[n] == "Wk" else st_v
                        for k in range(KT):
                            last = pe.transpose(bank[:, k * P:(k + 1) * P], st[:, k * P:(k + 1) * P], ident[:, :])
                    elif SETUP[n] == "mask":
                        pe.wait_ge(masks_f, 1)
                        for kt in range(TT):
                            for t in range(TT):
                                last = pe.transpose(bank[:, kt * L + t * P:kt * L + (t + 1) * P],
                                                    mask_f[:, t, kt * P:(kt + 1) * P], ident[:, :])
                    elif SETUP[n] == "columns":
                        pe.wait_ge(rows_f, 1)
                        rows = row_us + FT
                        last = pe.transpose(bank[:, 0:rows], rows_in[:, :], ident[0:rows, 0:rows])
                    else:
                        k = int(SETUP[n][2])
                        for t in range(KT):
                            last = pe.transpose(bank[:, t * P:(t + 1) * P], st_q[:, t, k * P:(k + 1) * P],
                                                ident[:, :])
                    last.then_inc(set_ready, 1)

            def work_bank(piece, b):
                for chain, count in bank_waits(piece, b).items():
                    past(pe, {"a": a_free, "b": b_free, "c": c_free}[chain], count)
                return work[BANK[piece]]

            def maxima(b, g, t, p_, k):
                if g == 0 and t == 0:
                    pe.wait_ge(qs_in, 96 * (b + 1))
                    pe.wait_ge(ks_in, 96 * (b + 1))
                    if isinstance(b, int) and b == 0:
                        pe.wait_ge(set_free, len(SETUP))
                past(pe, m_free, 16 * b + 2 * g - 1 + t)
                past(pe, t_free, 16 * (b - 1) + 2 * (g + 2) + t + 1 if g < 6 else 16 * b + 2 * (g - 6) + t + 1)
                for j in range(HPG):
                    pair, at = 2 * g + j // 2, 64 * (j % 2)
                    last = mm(sc[k][:, place(j)], qs[p_][at:at + 3 * HD, pair, t * P:(t + 1) * P],
                              ks[p_][at:at + 3 * HD, g, :], start=True, stop=True)
                last.then_inc(m_ready, 1)

            def scores(b, g, kt, p_):
                if g in (0, 4) and kt == 0:
                    pe.wait_ge(mr_in, 64 * (2 * b + g // 4 + 1))
                past(pe, t_free, 16 * b + 2 * g + kt - 1)
                done = 16 * b + 2 * (g + 5) + kt + 1
                past(pe, m_free, min(done, 16 * NB) if isinstance(done, int) else done)
                for j in range(HPG):
                    pair, at = 2 * g + j // 2, 64 * (j % 2)
                    last = mm(sc[kt][:, place(j)], ks[p_][at:at + 3 * HD + 2, g, kt * P:(kt + 1) * P],
                              qs[p_][at:at + 3 * HD + 2, pair, :], start=True, stop=True)
                last.then_inc(t_ready, 1)

            def weighted(b, g, kt, p_):
                pe.wait_ge(exp_done, 16 * b + 2 * g + kt + 1)
                if kt == 0:
                    past(pe, un_ready, 8 * b + g)
                    rows = 2 * b + (1 if g < ROWS_AT[0] else 2 if g < ROWS_AT[1] else 3)
                    past(pe, mr_high, min(rows, 2 * NB) if isinstance(rows, int) else rows)
                for j in range(HPG):
                    last = mm(av[32 * j:32 * (j + 1), 0:L], va[p_][:, kt, g, :],
                              ws[:, 2 * (g % 2) + kt, 2 * (j % 2) + j // 2, :], start=kt == 0, stop=kt == TT - 1)
                if kt == TT - 1:
                    last.then_inc(av_ready, 1)

            def piece(name, n, b):
                if name == "xT":
                    if n == 0:
                        pe.wait_ge(normed[0], 2 * (b + 1))
                    bank = work_bank((name, n), b)
                    for i in range(2):
                        for t in range(TT):
                            last = pe.transpose(bank[:, L * i + P * t:L * i + P * (t + 1)],
                                                xn[:, t, (2 * n + i) * P:(2 * n + i + 1) * P], ident[:, :])
                    last.then_inc(a_ready, 1)
                if name == "q":
                    if isinstance(b, int) and b == 0 and n == 0:
                        pe.wait_ge(set_free, 6)
                    pe.wait_ge(a_free, A_USES * b + A_PLACE["xT", 1])
                    bank = work_bank((name, n), b)
                    for i in range(2):
                        cols = slice((2 * n + i) * P, (2 * n + i + 1) * P)
                        for k in range(KT):
                            for s, (w, d) in enumerate(three(wq_h, wq_l, xh, xl)):
                                last = mm(bank[:, L * i:L * (i + 1)], w[:, k, cols], d[:, k, :],
                                          start=k == 0 and s == 0, stop=k == KT - 1 and s == 2)
                    last.then_inc(a_ready, 1)
                if name == "cT":
                    if n == 0:
                        pe.wait_ge(ld_c, 16 * (b + 1))
                    bank = work_bank((name, n), b)
                    for i in range(2):
                        for t in range(TT):
                            last = pe.transpose(bank[:, L * i + P * t:L * i + P * (t + 1)],
                                                cin[:, t, (2 * n + i) * P:(2 * n + i + 1) * P], ident[:, :])
                    last.then_inc(a_ready, 1)
                if name == "k":
                    if isinstance(b, int) and b == 0:
                        pe.wait_ge(set_free, 1)
                    pe.wait_ge(a_free, A_USES * b + A_PLACE["cT", 1])
                    bank = work_bank((name, n), b)
                    for k in range(KT):
                        for s, (w, d) in enumerate(three(wk_h, wk_l, ch, cl)):
                            last = mm(bank[:, 0:L], w[:, k, :], d[:, k, :], start=k == 0 and s == 0,
                                      stop=k == KT - 1 and s == 2)
                    last.then_inc(a_ready, 1)
                if name == "v":
                    if isinstance(b, int) and b == 0:
                        pe.wait_ge(set_free, 7)
                    bank = work_bank((name, n), b)
                    for t in range(TT):
                        for k in range(KT):
                            for s, (w, d) in enumerate(three(wv_h, wv_l, ch, cl)):
                                last = mm(bank[:, KV * t:KV * (t + 1)], d[:, k, t * P:(t + 1) * P], w[:, k, :],
                                          start=k == 0 and s == 0, stop=k == KT - 1 and s == 2)
                    last.then_inc(a_ready, 1)
                if name == "mrow":
                    pe.wait_ge(m_free, 16 * b + 8 * (n + 1))
                    past(pe, un_ready, 8 * b + ROWS_AT[0] if n == 1 else 8 * (b - 1) + ROWS_AT[1])
                    for t in range(TT):
                        last = pe.transpose(av[0:H // 2, P * t:P * (t + 1)], mx[:, t, 16 * n:16 * (n + 1)],
                                            ident[:, :])
                    last.then_inc(mr_ready, 1)
                if name == "spread":
                    if n == 0:
                        pe.wait_ge(rd_ready, b + 1)
                    bank = work_bank((name, n), b)
                    for i in range(2):
                        last = mm(bank[:, L * i:L * (i + 1)], spread[:, 2 * n + i, :], rd[:, :], start=True,
                                  stop=True)
                    last.then_inc(b_ready, 1)
                if name == "out":
                    if n == 0:
                        pe.wait_ge(at_ready, 2 * (b + 1))
                    bank = work_bank((name, n), b)
                    for k in range(KT):
                        for s, (d, w) in enumerate(((at_h, wo_h), (at_h, wo_l), (at_l, wo_h))):
                            last = mm(bank[:, :], d[:, k, n * P:(n + 1) * P], w[:, k, :], start=k == 0 and s == 0,
                                      stop=k == KT - 1 and s == 2)
                    last.then_inc(b_ready, 1)
                if name == "x2T":
                    if n == 0:
                        pe.wait_ge(normed[1], 2 * (b + 1))
                    bank = work_bank((name, n), b)
                    for i in range(2):
                        for t in range(TT):
                            last = pe.transpose(bank[:, L * i + P * t:L * i + P * (t + 1)],
                                                x2n[:, t, (2 * n + i) * P:(2 * n + i + 1) * P], ident[:, :])
                    last.then_inc(b_ready, 1)
                if name == "gu":
                    if n == 0 and isinstance(b, int) and b == 0:
                        pe.wait_ge(f8_done, len(slabs))
                    if n == 0:
                        pe.wait_ge(b_free, B_USES * b + 6)
                    bank = work_bank((name, n), b)
                    if not isinstance(b, int):
                        pe.sem_inc(pe_passed, 1)
                    for i, w in enumerate((wg8, wu8)):
                        for k in range(KT):
                            for s, d in enumerate((h2_h, h2_l)):
                                last = mm(bank[:, L * i:L * (i + 1)], w[:, k, n * P:(n + 1) * P], d[:, k, :],
                                          start=k == 0 and s == 0, stop=k == KT - 1 and s == 1)
                    last.then_inc(c_ready, 1)
                if name in ("down_a", "down_b"):
                    half = name == "down_b"
                    bank = work[BANK["down", n]] if half else work_bank(("down", n), b)
                    if n == 0:
                        pe.wait_ge(fl_ready, RING + FT * b + (FT if half else FT // 2))
                    if not isinstance(b, int):
                        pe.sem_inc(pe_passed, 1)
                    for c in range(FT // 2 * half, FT // 2 * (half + 1)):
                        for s, d in enumerate((f_h, f_l)):
                            last = mm(bank[:, :], d[:, c, n * P:(n + 1) * P], wd8[:, c, :], start=c == 0 and s == 0,
                                      stop=c == FT - 1 and s == 1)
                    if half:
                        last.then_inc(c_ready, 1)

            def steps(r, par):
                for step in range(STEPS):
                    u, k = step // 4, step % 4
                    if isinstance(r, int) and r == -2 and step in SETUP_AT:
                        set_up(*SETUP_AT[step])
                    unit = m_unit(r, step)
                    if unit is not None:
                        off, g, t = unit
                        maxima(r + off, g, t, par if off == 0 else 1 - par, k)
                    if k > 1 and there(r, 0):
                        scores(r, u, k - 2, par)
                    if k in SUMS_AT and u == 0 and there(r, -1):
                        weighted(r - 1, 7, SUMS_AT.index(k), 1 - par)
                    if k in SUMS_AT and u > 0 and there(r, 0):
                        weighted(r, u - 1, SUMS_AT.index(k), par)
                    for name, n, b, odd in pieces(r, par, step):
                        piece(name, n, b)

            iterations(pe, steps)


_INS = ["x", "ctx_2048", "mask_SxS2_bc0", "mask_BxS2_bk0", "g_xattn", "g_ffn", "L0_xattn_Wq", "L0_xattn_bq",
        "L0_xattn_Wk", "L0_xattn_bk", "L0_xattn_Wv", "L0_xattn_bv", "L0_xattn_Wo", "L0_xattn_bo", "L0_ffn_gate_w",
        "L0_ffn_up_w", "L0_ffn_down_w", "L0_ffn_gate_scale", "L0_ffn_up_scale", "L0_ffn_down_scale"]


def kernel(**inputs):
    import numpy as np
    import concourse.bacc as bacc
    from concourse.bass_utils import run_bass_kernel_spmd

    nc = bacc.Bacc("TRN2", target_bir_lowering=False, num_devices=1)
    arrays, args = {}, []
    to = np.zeros((2, H, KT, P), np.float16)
    for g in range(G):
        for j in range(HPG):
            at = 64 * (g % 2) + HD * j
            to[:, j * G + g, g // 2, at:at + HD] = 1.0
    consts = {"ident": np.eye(P, dtype=np.float32), "spread": to.reshape(2 * H, KT, P)}
    for name in _INS + list(consts):
        a = np.ascontiguousarray(inputs[name] if name in inputs else consts[name])
        if a.dtype == np.bool_:
            a = a.view(np.uint32)
        arrays[f"in_{name}"] = a
        args.append(nc.dram_tensor(f"in_{name}", a.shape, mybir.dt.from_np(a.dtype), kind="ExternalInput").ap())
    args.append(nc.dram_tensor("out_x", (NB, L, D), mybir.dt.float32, kind="ExternalOutput").ap())
    xattn_ffn(nc, *args)
    r = run_bass_kernel_spmd(nc, [arrays], core_ids=[0])
    return r.results[0]["out_x"]
```
